# Optimizing a Trainium2 kernel written in Bass

```python
import numpy as np
import jax
import jax.numpy as jnp

def _softmax(x, axis=-1):
    return jax.nn.softmax(x, axis=axis)

def _gelu(x):
    return jax.nn.gelu(x, approximate=True)

def _silu(x):
    return jax.nn.silu(x)

def _sigmoid(x):
    return jax.nn.sigmoid(x)

def _layernorm(x, axis=-1, eps=1e-05):
    m = jnp.mean(x, axis=axis, keepdims=True)
    v = jnp.var(x, axis=axis, keepdims=True)
    return (x - m) / jnp.sqrt(v + eps)

def _scatter_add(tgt, idx, src, axis=0):
    return tgt.at[idx].add(src)

def _segment_sum(src, seg, n):
    return jax.ops.segment_sum(src, seg, n)
kernel_name = 'mk_sandwich_d1_jaxref_r8_f4bb7b'

def setup_inputs(seed: int=0):
    np.random.seed(seed)
    _w = jnp.asarray

    def _L0_attn_setup():
        import jax, jax.numpy as jnp
        import numpy as np
        import math
        N_HEADS = 16
        ROPE_BASE = 10000.0

        def _rope_interleaved(t, cos, sin):
            te, to = (t[..., 0::2], t[..., 1::2])
            re = te * cos - to * sin
            ro = te * sin + to * cos
            return jnp.stack([re, ro], axis=-1).reshape(t.shape)
        key = jax.random.key(seed)
        ks = jax.random.split(key, 5)
        B, T, C = (2, 256, 128)
        s = 1.0 / math.sqrt(C)
        return {'x': jax.random.normal(ks[0], (B, T, C), dtype=jnp.float32), 'W_qkv': jax.random.normal(ks[1], (C, 3 * C), dtype=jnp.float32) * s, 'b_qkv': jax.random.normal(ks[2], (3 * C,), dtype=jnp.float32) * 0.02, 'W_proj': jax.random.normal(ks[3], (C, C), dtype=jnp.float32) * s, 'b_proj': jax.random.normal(ks[4], (C,), dtype=jnp.float32) * 0.02}
    _L0_attn_in = _L0_attn_setup()

    def _L0_ffn_setup():
        import jax, jax.numpy as jnp
        import numpy as np
        B, S, H, NH, E, F = (4, 128, 128, 16, 8, 512)
        D = H // NH
        EPS = 1e-05

        def _layernorm(x, g, b):
            mu = jnp.mean(x, axis=-1, keepdims=True)
            var = jnp.var(x, axis=-1, keepdims=True)
            return (x - mu) * jax.lax.rsqrt(var + EPS) * g + b
        key = jax.random.key(seed)
        ks = jax.random.split(key, 16)
        s = 0.02
        return {'x': jax.random.normal(ks[0], (B, S, H), jnp.float32), 'ln1_g': jnp.ones((H,), jnp.float32), 'ln1_b': jnp.zeros((H,), jnp.float32), 'ln2_g': jnp.ones((H,), jnp.float32), 'ln2_b': jnp.zeros((H,), jnp.float32), 'wq': jax.random.normal(ks[1], (H, H), jnp.float32) * s, 'bq': jnp.zeros((H,), jnp.float32), 'wk': jax.random.normal(ks[2], (H, H), jnp.float32) * s, 'bk': jnp.zeros((H,), jnp.float32), 'wv': jax.random.normal(ks[3], (H, H), jnp.float32) * s, 'bv': jnp.zeros((H,), jnp.float32), 'wo': jax.random.normal(ks[4], (H, H), jnp.float32) * s, 'bo': jnp.zeros((H,), jnp.float32), 'gate_w': jax.random.normal(ks[5], (H, E), jnp.float32) * s, 'gate_b': jnp.zeros((E,), jnp.float32), 'w1': jax.random.normal(ks[6], (E, H, F), jnp.float32) * s, 'b1': jnp.zeros((E, F), jnp.float32), 'w2': jax.random.normal(ks[7], (E, F, H), jnp.float32) * s, 'b2': jnp.zeros((E, H), jnp.float32)}
    _L0_ffn_in = _L0_ffn_setup()
    _d = {'L0_attn_x': _L0_attn_in['x'], 'L0_attn_W_qkv': _L0_attn_in['W_qkv'], 'L0_attn_b_qkv': _L0_attn_in['b_qkv'], 'L0_attn_W_proj': _L0_attn_in['W_proj'], 'L0_attn_b_proj': _L0_attn_in['b_proj'], 'L0_ffn_ln1_g': _L0_ffn_in['ln1_g'], 'L0_ffn_ln1_b': _L0_ffn_in['ln1_b'], 'L0_ffn_ln2_g': _L0_ffn_in['ln2_g'], 'L0_ffn_ln2_b': _L0_ffn_in['ln2_b'], 'L0_ffn_wq': _L0_ffn_in['wq'], 'L0_ffn_bq': _L0_ffn_in['bq'], 'L0_ffn_wk': _L0_ffn_in['wk'], 'L0_ffn_bk': _L0_ffn_in['bk'], 'L0_ffn_wv': _L0_ffn_in['wv'], 'L0_ffn_bv': _L0_ffn_in['bv'], 'L0_ffn_wo': _L0_ffn_in['wo'], 'L0_ffn_bo': _L0_ffn_in['bo'], 'L0_ffn_gate_w': _L0_ffn_in['gate_w'], 'L0_ffn_gate_b': _L0_ffn_in['gate_b'], 'L0_ffn_w1': _L0_ffn_in['w1'], 'L0_ffn_b1': _L0_ffn_in['b1'], 'L0_ffn_w2': _L0_ffn_in['w2'], 'L0_ffn_b2': _L0_ffn_in['b2']}
    _x0 = _d['L0_attn_x']
    _d['L0_attn_x'] = jax.random.normal(jax.random.fold_in(jax.random.key(seed), 1), (4, 1024, 128), dtype=_x0.dtype)
    del _x0
    return _d

def reference(L0_attn_x, L0_attn_W_qkv, L0_attn_b_qkv, L0_attn_W_proj, L0_attn_b_proj, L0_ffn_ln1_g, L0_ffn_ln1_b, L0_ffn_ln2_g, L0_ffn_ln2_b, L0_ffn_wq, L0_ffn_bq, L0_ffn_wk, L0_ffn_bk, L0_ffn_wv, L0_ffn_bv, L0_ffn_wo, L0_ffn_bo, L0_ffn_gate_w, L0_ffn_gate_b, L0_ffn_w1, L0_ffn_b1, L0_ffn_w2, L0_ffn_b2):

    def _L0_attn_ref(x, W_qkv, b_qkv, W_proj, b_proj):
        import jax, jax.numpy as jnp
        import numpy as np
        import math
        N_HEADS = 16
        ROPE_BASE = 10000.0

        def _rope_interleaved(t, cos, sin):
            te, to = (t[..., 0::2], t[..., 1::2])
            re = te * cos - to * sin
            ro = te * sin + to * cos
            return jnp.stack([re, ro], axis=-1).reshape(t.shape)
        B, T, C = x.shape
        H = N_HEADS
        dk = C // H
        qkv = x @ W_qkv + b_qkv
        q, k, v = jnp.split(qkv, 3, axis=-1)
        q = q.reshape(B, T, H, dk).transpose(0, 2, 1, 3)
        k = k.reshape(B, T, H, dk).transpose(0, 2, 1, 3)
        v = v.reshape(B, T, H, dk).transpose(0, 2, 1, 3)
        freqs = ROPE_BASE ** (-2.0 * jnp.arange(dk // 2, dtype=jnp.float32) / dk)
        angles = jnp.arange(T, dtype=jnp.float32)[:, None] * freqs[None, :]
        cos, sin = (jnp.cos(angles), jnp.sin(angles))
        q = _rope_interleaved(q, cos, sin)
        k = _rope_interleaved(k, cos, sin)
        attn = jnp.einsum('bhqd,bhkd->bhqk', q, k) / math.sqrt(dk)
        causal = jnp.triu(jnp.full((T, T), -jnp.inf, dtype=attn.dtype), k=1)
        attn = jax.nn.softmax(attn + causal, axis=-1)
        scores = jnp.einsum('bhqk,bhkd->bhqd', attn, v)
        scores = scores.transpose(0, 2, 1, 3).reshape(B, T, C)
        return scores @ W_proj + b_proj

    def _L0_ffn_ref(x, ln1_g, ln1_b, ln2_g, ln2_b, wq, bq, wk, bk, wv, bv, wo, bo, gate_w, gate_b, w1, b1, w2, b2):
        import jax, jax.numpy as jnp
        import numpy as np
        B, S, H, NH, E, F = (4, 128, 128, 16, 8, 512)
        D = H // NH
        EPS = 1e-05

        def _layernorm(x, g, b):
            mu = jnp.mean(x, axis=-1, keepdims=True)
            var = jnp.var(x, axis=-1, keepdims=True)
            return (x - mu) * jax.lax.rsqrt(var + EPS) * g + b
        b, s, h = x.shape
        hn = _layernorm(x, ln1_g, ln1_b)
        q = (hn @ wq + bq).reshape(b, s, NH, D).transpose(0, 2, 1, 3)
        k = (hn @ wk + bk).reshape(b, s, NH, D).transpose(0, 2, 1, 3)
        v = (hn @ wv + bv).reshape(b, s, NH, D).transpose(0, 2, 1, 3)
        scores = jnp.einsum('bhqd,bhkd->bhqk', q, k) / jnp.sqrt(jnp.float32(D))
        attn = jax.nn.softmax(scores, axis=-1)
        o = jnp.einsum('bhqk,bhkd->bhqd', attn, v)
        o = o.transpose(0, 2, 1, 3).reshape(b, s, h)
        x = x + (o @ wo + bo)
        hn2 = _layernorm(x, ln2_g, ln2_b).reshape(-1, h)
        logits = hn2 @ gate_w + gate_b
        idx = jnp.argmax(logits, axis=-1)
        mid = jax.nn.relu(jnp.einsum('th,ehf->etf', hn2, w1) + b1[:, None, :])
        y = jnp.einsum('etf,efh->eth', mid, w2) + b2[:, None, :]
        moe = y[idx, jnp.arange(hn2.shape[0])]
        return x + moe.reshape(b, s, h)
    x = L0_attn_x
    x = x + _layernorm(_L0_attn_ref(_layernorm(x, axis=-1), L0_attn_W_qkv, L0_attn_b_qkv, L0_attn_W_proj, L0_attn_b_proj), axis=-1)
    x = x + _layernorm(_L0_ffn_ref(_layernorm(x, axis=-1), L0_ffn_ln1_g, L0_ffn_ln1_b, L0_ffn_ln2_g, L0_ffn_ln2_b, L0_ffn_wq, L0_ffn_bq, L0_ffn_wk, L0_ffn_bk, L0_ffn_wv, L0_ffn_bv, L0_ffn_wo, L0_ffn_bo, L0_ffn_gate_w, L0_ffn_gate_b, L0_ffn_w1, L0_ffn_b1, L0_ffn_w2, L0_ffn_b2), axis=-1)
    return x

_drawn_inputs = setup_inputs


def setup_inputs(seed=0):
    import zlib

    import numpy as np

    out = dict(_drawn_inputs(seed))
    spreads = {'L0_ffn_ln1_g': (1.0, 0.6),
     'L0_ffn_ln1_b': (0.0, 0.8),
     'L0_ffn_ln2_g': (1.0, 0.58),
     'L0_ffn_ln2_b': (0.0, 0.468),
     'L0_ffn_bq': (0.0, 0.8),
     'L0_ffn_bk': (0.0, 2.0),
     'L0_ffn_bv': (0.0, 0.603),
     'L0_ffn_bo': (0.0, 0.1),
     'L0_ffn_gate_b': (0.0, 0.1),
     'L0_ffn_b1': (0.0, 0.644),
     'L0_ffn_b2': (0.0, 0.337)}
    factors = {'L0_ffn_wq': 8.0, 'L0_ffn_wk': 8.0, 'L0_ffn_wv': 5.15, 'L0_ffn_wo': 3.508}
    for name, (base, spread) in spreads.items():
        noise = np.random.default_rng([zlib.crc32(name.encode()), seed]).standard_normal(out[name].shape)
        drawn = base * np.exp(spread * noise) if base else spread * noise
        out[name] = jnp.asarray(drawn.astype(out[name].dtype))
    for name, factor in factors.items():
        out[name] = (out[name] * factor).astype(out[name].dtype)
    return out
```

```python
from contextlib import ExitStack

import numpy as np

import concourse.bass as bass
from concourse import mybir

F32 = mybir.dt.float32
BF16 = mybir.dt.bfloat16
U32 = mybir.dt.uint32
ALU = mybir.AluOpType
ACT = mybir.ActivationFunctionType
AX = mybir.AxisListType

P = 128
B, T, C = 4, 1024, 128
H, D = 16, 8
E, F = 8, 512
NT = T // P
G = 4
HG = H // G
HALF = 512
NPART = 3
STACK = NPART * NPART * D
MROW = 96
KROWS = MROW + NPART
SCALE = float(D) ** -0.5
EPS = 1e-5
NEG = -3.0e38


def attend_steps(causal):
    out = []
    for half in range(T // HALF):
        for kt in range(NT):
            if causal and kt * P >= (half + 1) * HALF:
                continue
            off = max(0, kt * P - half * HALF) if causal else 0
            out.append((half, kt, off, causal and kt * P >= half * HALF))
    return out


def max_units(causal):
    return [(j, qt, P * (qt + 1) if causal else T) for half in range(2) for j in range(HG)
            for qt in range(half * NT // 2, (half + 1) * NT // 2)]


SLOTTED = ("max", "turn", "side")


def plan(a, prep, post):
    before_q = ["stats n1", "norm n1"] + (["stats n2", "norm n2"] if prep == 2 else [])
    side = {}
    if post:
        side[0, 0] = [("rec",)]
        side[0, 2] = [("side", "proj")] + ([("stats", "post")] if post == 1 else [])
        side[0, 4] = ([("norm", "post")] if post == 1 else []) + [("add",)]
        side[0, 9] = [("out", "res")]
    if prep:
        for n, what in enumerate(before_q):
            side[0, 5 + n] = [tuple(what.split())]
        side[0, 9] = side.get((0, 9), []) + [("side", "xt")]
        side[0, 10] = [("side", "q")]
        side[0, 11] = ([("side", "qs")] if prep == 1 else []) + [("cut", "q")]
        side[1, 2] = [("out", "q")] + ([("out", "xn")] if prep == 2 else [])
        side[1, 3] = [("side", "k")]
        side[1, 4] = ([("side", "ks")] if prep == 1 else []) + [("cut", "k")]
        side[1, 6] = [("side", "v")]
        side[2, 2] = [("out", "k")]
        side[2, 3] = [("load", 0)]
        side[3, 2] = [("vg", 0), ("vg", 1), ("vg", 2), ("load", 1)]
        side[3, 4] = [("load", 2)]
    if a is None:
        items = [it for key in sorted(side) for it in side[key]]
        if prep:
            items += max_items(0, prep == 1)
        return [(None, [it]) for it in items]
    causal = a == 1
    side[0, 0] = [("load", G - 1), ("vg", G - 1)] + side.get((0, 0), [])
    for g in range(G):
        side[g, 1] = [("turn", 1, g)] + side.get((g, 1), [])
        if g:
            side[g, 3] = side.get((g, 3), []) + [("heads", g - 1)]
    steps = attend_steps(causal)
    pace = np.cumsum([HALF - off + 150 for _, _, off, _ in steps])
    ticks = []
    for g in range(G):
        todo = [side.get((g, s), []) for s in range(len(steps))]
        if prep or g < G - 1:
            causal_next = causal if g < G - 1 else prep == 1
            units = max_items((g + 1) % G, causal_next)
            cost = np.cumsum([0.0] + [keys + 100 for _, _, keys in max_units(causal_next)])
            s = 0
            for it in units:
                if it[0] == "max":
                    s = int(np.searchsorted(pace / pace[-1], (cost[it[2]] + cost[it[2] + 1]) / 2 / cost[-1]))
                todo[s] = todo[s] + [it]
        for s, (half, kt, off, diag) in enumerate(steps):
            last_kt = max(k for h, k, _, _ in steps if h == half)
            ticks.append(((g, half, kt, off, diag, last_kt, 2 * g + half), todo[s]))
    ticks.append((None, [("heads", G - 1)]))
    return ticks


def max_items(g, causal):
    items = []
    for u in range(HG * NT):
        items.append(("max", g, u, causal))
        if u % 16 == 15:
            items.append(("split", u // 16, g, items[-1]))
        if u == 19:
            items.append(("turn", 0, g))
    return items


def build_kernel(nc, x, wqs, wks, wq1, wk1, wv1, bq1, bqs, bk1, bks, bv1, wp1, bp1,
                 ln1g, ln1b, ln2g, ln2b, wq2, wk2, wv2, bq2, bk2, bv2, wo2, bo2,
                 gate_w, gate_b, w1, b1, w2, b2, cos, sin, ident, causal_q, causal_k, iota_e, out):
    x_t = x.rearrange("b (t p) c -> b p t c", p=P)
    out_t = out.rearrange("b (t p) c -> b p t c", p=P)

    def scratch(name, shape, dt):
        return nc.dram_tensor(name, shape, dt, kind="Internal").ap()

    q_d = scratch("q_scratch", [NPART, 2, P, HALF], BF16)
    k_d = scratch("k_scratch", [NPART, P, T], BF16)
    x1_d = scratch("x1_scratch", [B, P, NT, C], F32)
    xn_d = scratch("xn_scratch", [B, P, NT, C], F32)
    xa_d = scratch("xa_scratch", [B, P, NT, C], F32)

    with ExitStack() as whole:
        def sem(name, ctx=whole):
            return ctx.enter_context(nc.semaphore(name))

        def sb(name, shape, dt=F32, ctx=whole):
            return ctx.enter_context(nc.sbuf_tensor(name, shape, dt))

        idf = sb("idf", [P, P])
        wgt = {n: sb(f"w_{n}", [P, C]) for n in ("q1", "qs1", "k1", "ks1", "v1", "o1", "q2", "k2", "v2", "o2")}
        col = sb("col", [P, 10])
        rows = sb("rows", [P, 4, C])
        XT = sb("XT", [P, T])
        XIN = sb("XIN", [P, NT, C])
        XH = sb("XH", [P, NT, C])
        XH2 = sb("XH2", [P, NT, C])
        Y = sb("Y", [P, NT, C])
        RES = sb("RES", [P, NT, C])
        st6 = sb("st6", [P, NT, 6])
        mv = sb("mv", [P, NT, 2])
        rstd = sb("rstd", [P, NT])
        halfneg = sb("halfneg", [P, NT])
        BQ1, BQS, BK1, BKS, BQ2, BK2, G1, B1, G2, B2 = range(10)

        s_load = sem("s_load")
        s_init = sem("s_init")
        s_zero = sem("s_zero")

        iteration_sems = []

        def isem(name):
            iteration_sems.append(sem(name))
            return iteration_sems[-1]

        slot_full = [isem(f"slot_full{n}") for n in range(2)]
        slot_free = [isem(f"slot_free{n}") for n in range(2)]
        st_full = isem("st_full")
        exp_done = isem("exp_done")
        av_done = isem("av_done")
        o_evacuated = isem("o_evacuated")
        max_split = isem("max_split")
        rows_in = [isem(f"rows_in{n}") for n in range(2)]
        xin_in, res_in, xn_out, res_out = isem("xin_in"), isem("res_in"), isem("xn_out"), isem("res_out")
        stats_done, rstd_done, norm_done = isem("stats_done"), isem("rstd_done"), isem("norm_done")
        split_done, parts_out = isem("split_done"), isem("parts_out")
        vg_done = isem("vg_done")
        stack_in = [isem(f"stack_in{g}") for g in range(G)]
        heads_in = [isem(f"heads_in{n}") for n in range(2)]
        rec_done, at_done, res_done = isem("rec_done"), isem("at_done"), isem("res_done")
        pool_chain, dve_chain = isem("pool_chain"), isem("dve_chain")
        w_in, routed, route_sb = isem("w_in"), isem("routed"), isem("route_sb")
        h_full, h_done, y_full, y_used, y_added = (isem(n) for n in ("h_full", "h_done", "y_full", "y_used", "y_added"))
        out_done = isem("out_done")

        def end_iteration():
            nc.all_engine_barrier(sems_to_clear=range(iteration_sems[0].num, iteration_sems[-1].num + 1))

        loads = [(idf[:], ident), (wgt["o1"][:], wp1), (wgt["o2"][:], wo2),
                 (wgt["q1"][:], wq1), (wgt["qs1"][:], wqs), (wgt["k1"][:], wk1), (wgt["ks1"][:], wks),
                 (wgt["v1"][:], wv1), (wgt["q2"][:], wq2), (wgt["k2"][:], wk2), (wgt["v2"][:], wv2)]
        for n, v in enumerate((bq1, bqs, bk1, bks, bq2, bk2, ln1g, ln1b, ln2g, ln2b)):
            loads.append((col[:, n:n + 1], v.rearrange("(c o) -> c o", o=1)))
        for n, v in enumerate((bv1, bp1, bv2, bo2)):
            loads.append((rows[:, n, :], v.rearrange("(o c) -> o c", o=1).to_broadcast([P, C])))

        att = ExitStack()
        QS = [sb(f"QS{g}", [KROWS, 2, HG, HALF], BF16, att) for g in range(G)]
        KS = [sb(f"KS{g}", [KROWS, HG, T], BF16, att) for g in range(G)]
        VG = [sb(f"VG{g}", [P, NT, HG, 32], F32, att) for g in range(G)]
        PT = sb("PT", [P, 2, HG, HALF], F32, att)
        OT = sb("OT", [P, 2, T], F32, att)
        NUM = sb("NUM", [P, T], F32, att)
        DEN = sb("DEN", [P, T], F32, att)
        T1 = sb("T1", [P, T], F32, att)
        T2 = sb("T2", [P, T], F32, att)
        parts = sb("parts", [P, NPART, T], BF16, att)
        cos_sb = sb("cos_sb", [P, T], F32, att)
        sin_sb = sb("sin_sb", [P, T], F32, att)
        VST = sb("VST", [P, NT, C], F32, att)
        idb = sb("idb", [P, P], BF16, att)
        mask_q = sb("mask_q", [P, P], BF16, att)
        mask_k = sb("mask_k", [P, P], BF16, att)
        NM = sb("NM", [P, 2, 16], F32, att)
        NMR = sb("NMR", [P, 2, 16], F32, att)
        NMP = sb("NMP", [P, 2, NPART, 16], BF16, att)
        NMT = sb("NMT", [NPART * 16, 2, P], BF16, att)
        slots = [att.enter_context(nc.psum_tensor(f"slot{n}", [P, T], F32)) for n in range(2)]
        stb = att.enter_context(nc.psum_tensor("stb", [P, 3, HALF], F32))
        OB = att.enter_context(nc.psum_tensor("OB", [P, HALF], F32))
        AT = sb("AT", [P, T], F32, att)
        loads += [(cos_sb[:], cos), (sin_sb[:], sin), (mask_q[:], causal_q), (mask_k[:], causal_k)]

        with nc.Block() as block:
            @block.sync
            def _(sp):
                for dst, src in loads:
                    sp.dma_start(dst, src).then_inc(s_load, 16)
                sp.wait_ge(s_load, 16 * len(loads))

            @block.vector
            def _(dve):
                for g in range(G):
                    nc.vector.memset(QS[g][64:MROW], 0.0)
                    nc.vector.memset(KS[g][64:MROW, :, :], 0.0)
                    nc.vector.memset(KS[g][MROW:KROWS, :, :], 1.0)
                nc.vector.memset(halfneg[:], -0.5).then_inc(s_init, 1)
                dve.wait_ge(s_load, 16 * len(loads))
                nc.vector.tensor_copy(idb[:], idf[:]).then_inc(s_init, 1)

            @block.gpsimd
            def _(pool):
                for g in range(G):
                    nc.gpsimd.memset(VG[g][:, :, :, D:2 * D], 1.0)
                    nc.gpsimd.memset(VG[g][:, :, :, 2 * D:32], 0.0).then_inc(s_zero, 1)
        nc.all_engine_barrier()


        def iteration(a=None, prep=None, prep_b=None, post=None, post_b=None):
            ticks = plan(a, prep, post)
            order = [it for _, items in ticks for it in items if it[0] in SLOTTED]
            slot_use = {it: n for n, it in enumerate(order)}
            splits = [it for _, items in ticks for it in items if it[0] == "split"]
            turns = [it for it in order if it[0] == "turn"]
            n_steps = sum(step is not None for step, _ in ticks)
            per_group = n_steps // G

            def slot_of(it):
                return slot_use[it]

            def wait_slot_free(eng, it):
                n = slot_of(it)
                if n >= 2:
                    eng.wait_ge(slot_free[n % 2], n // 2)

            def wait_slot_full(eng, it):
                n = slot_of(it)
                eng.wait_ge(slot_full[n % 2], n // 2 + 1)

            def wait_slot_emptied(eng, it):
                n = slot_of(it)
                eng.wait_ge(slot_free[n % 2], n // 2 + 1)

            def emptied(ins, it):
                ins.then_inc(slot_free[slot_of(it) % 2], 1)

            def slot(it):
                return slots[slot_of(it) % 2]

            norms = [it[1] for _, items in ticks for it in items if it[0] == "stats"]
            norm_src = {"post": Y, "n1": XIN, "n2": XH}
            norm_dst = {"post": Y, "n1": XH, "n2": XH2}

            def units(it):
                return max_units(it[3])[it[2]]

            with nc.Block() as block:
                @block.sync
                def _(sp):
                    if prep:
                        sp.dma_start(XIN[:], x_t[prep_b] if prep == 1 else x1_d[prep_b]).then_inc(xin_in, 16)
                    if post:
                        sp.dma_start(RES[:], x_t[post_b] if post == 1 else xn_d[post_b]).then_inc(res_in, 16)
                    ends = {}

                    def load_stack(g):
                        hs = slice(HG * g, HG * g + HG)
                        for i in range(NPART):
                            kv = k_d.rearrange("j (d h) t -> (j d) h t", d=D)[:, hs, :]
                            sp.dma_start(KS[g][i * NPART * D:(i + 1) * NPART * D, :, :], kv).then_inc(stack_in[g], 16)
                            qv = q_d[i].rearrange("s (d h) t -> d s (h t)", d=D)[:, :, HG * g * HALF:HG * (g + 1) * HALF]
                            for j in range(NPART):
                                r = (i * NPART + j) * D
                                sp.dma_start(QS[g][r:r + D].rearrange("d s h t -> d s (h t)"), qv).then_inc(stack_in[g], 16)
                        ends[stack_in[g]] = 16 * NPART * (NPART + 1)

                    def heads_out(g):
                        sp.wait_ge(o_evacuated, 2 * (g + 1))
                        if g == 0 and post:
                            sp.wait_ge(at_done, 1)
                        for j in range(HG):
                            r = (HG * g + j) * D
                            sp.dma_start(NUM[r:r + D, :], OT[32 * j:32 * j + D, g % 2, :]).then_inc(heads_in[g % 2], 16)
                            sp.dma_start(DEN[r:r + D, :], OT[32 * j + D:32 * j + 2 * D, g % 2, :])\
                                .then_inc(heads_in[g % 2], 16)
                        ends[heads_in[g % 2]] = ends.get(heads_in[g % 2], 0) + 32 * HG

                    for _, items in ticks:
                        for it in items:
                            if it[0] == "turn":
                                _, half, g = it
                                wait_slot_emptied(sp, it)
                                for p in range(NPART):
                                    sp.dma_start(QS[g][MROW + p:MROW + p + 1, half],
                                                 NMT[p * 16:(p + 1) * 16, half, :]).then_inc(rows_in[half], 16)
                                ends[rows_in[half]] = ends.get(rows_in[half], 0) + 16 * NPART
                            elif it[0] == "load":
                                g = it[1]
                                if g < G - 1:
                                    sp.wait_ge(parts_out, 32)
                                    if a:
                                        sp.wait_ge(av_done, per_group * (g + 1))
                                load_stack(g)
                            elif it[0] == "heads":
                                heads_out(it[1])
                            elif it[0] == "out":
                                if it[1] == "res":
                                    sp.wait_ge(res_done, 1)
                                    sp.dma_start(x1_d[post_b] if post == 1 else xa_d[post_b], RES[:])\
                                        .then_inc(res_out, 16)
                                    ends[res_out] = 16
                                elif it[1] == "xn":
                                    sp.wait_ge(norm_done, norms.index("n1") + 1)
                                    sp.dma_start(xn_d[prep_b], XH[:]).then_inc(xn_out, 16)
                                    ends[xn_out] = 16
                                else:
                                    n = "qk".index(it[1])
                                    if it[1] == "q" and a:
                                        sp.wait_ge(stack_in[G - 1], 16 * NPART * (NPART + 1))
                                    sp.wait_ge(split_done, n + 1)
                                    dst, src = ((k_d.rearrange("j p t -> p j t"), parts[:]) if n else
                                                (q_d.rearrange("j s p t -> p (j s) t"),
                                                 parts[:].rearrange("p j (s t) -> p (j s) t", s=2)))
                                    sp.dma_start(dst, src).then_inc(parts_out, 16)
                                    ends[parts_out] = 16 * (n + 1)
                    for s, n in ends.items():
                        sp.wait_ge(s, n)

                @block.tensor
                def _(pe):
                    def do_max(it):
                        j, qt, keys = units(it)
                        g, causal = it[1], it[3]
                        if g in (0, G - 1):
                            pe.wait_ge(stack_in[g], 16 * NPART * (NPART + 1))
                        wait_slot_free(pe, it)
                        w = QS[g][0:MROW, qt // 4, j, qt % 4 * P:(qt % 4 + 1) * P]
                        at = qt * P if causal else T
                        if causal:
                            nc.tensor.matmul(slot(it)[:, at:at + P], w, KS[g][0:MROW, j, at:at + P],
                                             start=True, stop=False)
                            last = nc.tensor.matmul(slot(it)[:, at:at + P], idb[:], mask_q[:], start=False, stop=True)
                        for c in range(0, min(at, keys), HALF):
                            e = min(c + HALF, at)
                            last = nc.tensor.matmul(slot(it)[:, c:e], w, KS[g][0:MROW, j, c:e], start=True, stop=True)
                        last.then_inc(slot_full[slot_of(it) % 2], 1)

                    def do_turn(it):
                        half = it[1]
                        if (half, it[2]) != (1, 0) or a is None:
                            pe.wait_ge(max_split, [x[1:3] for x in splits].index((half, it[2])) + 1)
                        wait_slot_free(pe, it)
                        nc.tensor.transpose(slot(it)[0:NPART * 16, 0:P // 2].bitcast(BF16),
                                            NMP[:, half, :, :].rearrange("p a b -> p (a b)"), idb[:])\
                            .then_inc(slot_full[slot_of(it) % 2], 1)

                    def do_side(it):
                        name = it[1]
                        wait_slot_free(pe, it)
                        o = slot(it)
                        if name == "xt":
                            pe.wait_ge(norm_done, norms.index("n2" if prep == 2 else "n1") + 1)
                            src = XH2 if prep == 2 else XH
                            for t in range(NT):
                                last = nc.tensor.transpose(o[:, t * P:(t + 1) * P], src[:, t, :], idf[:])
                        elif name in ("q", "qs", "k", "ks"):
                            wait_slot_emptied(pe, ("side", "xt"))
                            for c in range(0, T, HALF):
                                last = nc.tensor.matmul(o[:, c:c + HALF], wgt[f"{name}{prep}"][:], XT[:, c:c + HALF],
                                                        start=True, stop=True)
                        elif name == "v":
                            wait_slot_emptied(pe, ("side", "xt"))
                            for t in range(NT):
                                last = nc.tensor.matmul(o[:, t * P:(t + 1) * P], XT[:, t * P:(t + 1) * P],
                                                        wgt[f"v{prep}"][:], start=True, stop=True)
                        elif name == "proj":
                            pe.wait_ge(at_done, 1)
                            for t in range(NT):
                                last = nc.tensor.matmul(o[:, t * P:(t + 1) * P], AT[:, t * P:(t + 1) * P],
                                                        wgt[f"o{post}"][:], start=True, stop=True)
                        last.then_inc(slot_full[slot_of(it) % 2], 1)

                    def item(it):
                        {"max": do_max, "turn": do_turn, "side": do_side}[it[0]](it)

                    def weigh(step, n):
                        g, half, kt, off, _, last_kt, chunk = step
                        pe.wait_ge(exp_done, HG * (n + 1))
                        if kt == 0 and chunk >= 1:
                            pe.wait_ge(o_evacuated, chunk)
                        if chunk == 2 * (G - 1) and kt == 0:
                            pe.wait_ge(vg_done, 1)
                        for j in range(HG):
                            last = nc.tensor.matmul(OB[32 * j:32 * j + 32, off:HALF], VG[g][:, kt, j, :],
                                                    PT[:, n % 2, j, off:HALF], start=(kt == 0), stop=(kt == last_kt),
                                                    skip_group_check=True)
                        last.then_inc(av_done, 1)

                    before = None
                    n = 0
                    for step, items in ticks:
                        mine = [it for it in items if it[0] in SLOTTED]
                        if step is None:
                            for it in mine:
                                item(it)
                            continue
                        g, half, kt, off, diag, last_kt, chunk = step
                        if kt == 0:
                            if g + half:
                                pe.wait_ge(rows_in[half], 16 * NPART * (g + half))
                        for j in range(HG):
                            m = HG * n + j
                            if m >= 3:
                                pe.wait_ge(exp_done, m - 2)
                            o = stb[:, m % 3, :]
                            w = KS[g][:, j, kt * P:(kt + 1) * P]
                            if diag:
                                nc.tensor.matmul(o[:, off:off + P], w, QS[g][:, half, j, off:off + P], start=True, stop=False)
                                last = nc.tensor.matmul(o[:, off:off + P], idb[:], mask_k[:], start=False, stop=True)
                                if off + P < HALF:
                                    last = nc.tensor.matmul(o[:, off + P:HALF], w,
                                                            QS[g][:, half, j, off + P:HALF], start=True, stop=True)
                            else:
                                last = nc.tensor.matmul(o[:, off:HALF], w, QS[g][:, half, j, off:HALF],
                                                        start=True, stop=True)
                            last.then_inc(st_full, 1)
                            if j == 1 and mine:
                                item(mine[0])
                        if before is not None:
                            weigh(before, n - 1)
                        for it in mine[1:]:
                            item(it)
                        before = step
                        n += 1
                    if before is not None:
                        weigh(before, n - 1)

                @block.scalar
                def _(act):
                    def evacuate(chunk):
                        g, half = divmod(chunk, 2)
                        if g >= 2 and half == 0:
                            act.wait_ge(heads_in[g % 2], 32 * HG)
                        nc.scalar.copy(OT[:, g % 2, half * HALF:(half + 1) * HALF], OB[:]).then_inc(o_evacuated, 1)

                    n = 0
                    done = None
                    for step, items in ticks:
                        if step is not None:
                            g, half, kt, off, diag, last_kt, chunk = step
                            for j in range(HG):
                                m = HG * n + j
                                act.wait_ge(st_full, m + 1)
                                if j == 0 and n >= 2:
                                    act.wait_ge(av_done, n - 1)
                                nc.scalar.activation(PT[:, n % 2, j, off:HALF], stb[:, m % 3, off:HALF], ACT.Exp,
                                                     scale=SCALE).then_inc(exp_done, 1)
                            if done is not None:
                                act.wait_ge(av_done, n)
                                evacuate(done)
                                done = None
                            if kt == last_kt:
                                done = chunk
                            n += 1
                        for it in items:
                            if it[0] == "turn":
                                wait_slot_full(act, it)
                                before = sum(x[1] == it[1] for x in turns[:turns.index(it)])
                                if before:
                                    act.wait_ge(rows_in[it[1]], 16 * NPART * before)
                                emptied(nc.scalar.copy(NMT[:, it[1], :],
                                                       slot(it)[0:NPART * 16, 0:P // 2].bitcast(BF16)), it)
                            elif it == ("side", "xt"):
                                wait_slot_full(act, it)
                                if prep == 1:
                                    emptied(nc.scalar.copy(XT[:], slot(it)[:]), it)
                                else:
                                    emptied(nc.scalar.activation(XT[:], slot(it)[:], ACT.Identity,
                                                                 bias=col[:, B1:B1 + 1], scale=col[:, G1:G1 + 1]), it)
                    if done is not None:
                        act.wait_ge(av_done, n)
                        evacuate(done)

                @block.vector
                def _(dve):
                    links = [0]

                    def link(ins):
                        links[0] += 1
                        ins.then_inc(dve_chain, 1)
                        dve.wait_ge(dve_chain, links[0])

                    for it in (it for _, items in ticks for it in items):
                        if it[0] == "max":
                            j, qt, keys = units(it)
                            half = it[2] // 16
                            if it[2] % 16 == 0:
                                before = [n for n, x in enumerate(splits) if x[1] == half
                                          and splits.index(next(y for y in splits if y[1:3] == (half, it[1]))) > n]
                                if before:
                                    dve.wait_ge(max_split, before[-1] + 1)
                            wait_slot_full(dve, it)
                            at = j * 4 + qt % 4
                            emptied(nc.vector.tensor_reduce(NM[:, half, at:at + 1], slot(it)[:, 0:keys], AX.X,
                                                            ALU.max, negate=True), it)
                        elif it[0] == "rec":
                            nc.vector.reciprocal(DEN[:], DEN[:]).then_inc(rec_done, 1)
                        elif it == ("side", "proj"):
                            wait_slot_full(dve, it)
                            bias = rows[:, 1 if post == 1 else 3, :].unsqueeze(1).to_broadcast([P, NT, C])
                            emptied(nc.vector.tensor_tensor(Y[:], slot(it)[:].rearrange("p (t c) -> p t c", t=NT),
                                                            bias, ALU.add), it)
                        elif it[0] == "stats":
                            src = norm_src[it[1]]
                            if it[1] == "post":
                                wait_slot_emptied(dve, ("side", "proj"))
                            elif it[1] == "n1":
                                dve.wait_ge(xin_in, 16)
                            else:
                                dve.wait_ge(norm_done, norms.index("n1") + 1)
                            for t in range(NT):
                                last = nc.vector.bn_stats(st6[:, t, :], src[:, t, :])
                            link(last)
                            for t in range(NT):
                                last = nc.vector.bn_aggr(mv[:, t, :], st6[:, t, :])
                            last.then_inc(stats_done, 1)
                        elif it[0] == "norm":
                            dve.wait_ge(rstd_done, norms.index(it[1]) + 1)
                            for t in range(NT):
                                last = nc.vector.tensor_scalar(norm_dst[it[1]][:, t, :], norm_src[it[1]][:, t, :],
                                                               mv[:, t, 0:1], rstd[:, t:t + 1],
                                                               ALU.subtract, ALU.mult)
                            last.then_inc(norm_done, 1)
                        elif it[0] == "side" and it[1] in ("q", "k", "qs", "ks"):
                            wait_slot_full(dve, it)
                            if it[1] == "k":
                                dve.wait_ge(split_done, 1)
                            c = {"q1": BQ1, "qs1": BQS, "k1": BK1, "ks1": BKS, "q2": BQ2, "k2": BK2}[f"{it[1]}{prep}"]
                            if prep == 1:
                                dst, table = (T2, sin_sb) if it[1][1:] else (T1, cos_sb)
                                emptied(nc.vector.scalar_tensor_tensor(dst[:], slot(it)[:], col[:, c:c + 1], table[:],
                                                                       ALU.add, ALU.mult), it)
                            else:
                                emptied(nc.vector.tensor_scalar(T1[:], slot(it)[:], col[:, c:c + 1], None, ALU.add), it)
                        elif it == ("side", "v"):
                            wait_slot_full(dve, it)
                            if a:
                                dve.wait_ge(vg_done, 1)
                            bias = rows[:, 0 if prep == 1 else 2, :].unsqueeze(1).to_broadcast([P, NT, C])
                            emptied(nc.vector.tensor_tensor(VST[:], slot(it)[:].rearrange("p (t c) -> p t c", t=NT),
                                                            bias, ALU.add), it)

                @block.gpsimd
                def _(pool):
                    links = [0]

                    def link(ins):
                        links[0] += 1
                        ins.then_inc(pool_chain, 1)
                        pool.wait_ge(pool_chain, links[0])

                    def split(src, rest, part, done):
                        link(nc.gpsimd.tensor_copy(part(0), src))
                        link(nc.gpsimd.tensor_tensor(rest, src, part(0), ALU.subtract))
                        link(nc.gpsimd.tensor_copy(part(1), rest))
                        nc.gpsimd.tensor_tensor(part(2), rest, part(1), ALU.subtract).then_inc(done, 1)

                    placed = 0
                    for it in (it for _, items in ticks for it in items):
                        if it[0] == "split":
                            _, half, g, last = it
                            wait_slot_emptied(pool, last)
                            before = [t for t in turns if t[1] == half and order.index(t) < order.index(last)]
                            if before:
                                wait_slot_full(pool, before[-1])
                            split(NM[:, half, :], NMR[:, half, :], lambda p: NMP[:, half, p, :], max_split)
                        elif it[0] == "vg":
                            g = it[1]
                            if g < G - 1:
                                wait_slot_emptied(pool, ("side", "v"))
                                if a:
                                    pool.wait_ge(av_done, per_group * (g + 1))
                            nc.gpsimd.tensor_copy(VG[g][:, :, :, 0:D],
                                                  VST[:, :, g * HG * D:(g + 1) * HG * D]
                                                  .rearrange("p t (j d) -> p t j d", d=D)).then_inc(vg_done, 1)
                        elif it[0] == "rec":
                            pool.wait_ge(rec_done, 1)
                            nc.gpsimd.tensor_tensor(AT[:], NUM[:], DEN[:], ALU.mult).then_inc(at_done, 1)
                        elif it[0] == "add":
                            pool.wait_ge(res_in, 16)
                            if post == 1:
                                pool.wait_ge(norm_done, norms.index("post") + 1)
                            else:
                                wait_slot_emptied(pool, ("side", "proj"))
                            nc.gpsimd.tensor_tensor(RES[:], RES[:], Y[:], ALU.add).then_inc(res_done, 1)
                        elif it[0] == "stats":
                            pool.wait_ge(stats_done, norms.index(it[1]) + 1)
                            link(nc.gpsimd.tensor_scalar(rstd[:], mv[:, :, 1], EPS, None, ALU.add))
                            nc.gpsimd.tensor_tensor(rstd[:], rstd[:], halfneg[:], ALU.pow).then_inc(rstd_done, 1)
                        elif it[0] == "cut":
                            wait_slot_emptied(pool, ("side", it[1]))
                            if prep == 1:
                                wait_slot_emptied(pool, ("side", it[1] + "s"))
                                link(nc.gpsimd.tensor_tensor(T1[:], T1[:], T2[:], ALU.add))
                            if it[1] == "k":
                                pool.wait_ge(parts_out, 16)
                            split(T1[:], T1[:], lambda p: parts[:, p, :], split_done)
            end_iteration()

        iteration(prep=1, prep_b=0)
        iteration(a=1, prep=1, prep_b=1)
        with nc.Fori(1, B - 1) as b:
            iteration(a=1, prep=1, prep_b=b + 1, post=1, post_b=b - 1)
        iteration(a=1, prep=2, prep_b=0, post=1, post_b=B - 2)
        iteration(a=2, prep=2, prep_b=1, post=1, post_b=B - 1)
        with nc.Fori(1, B - 1) as b:
            iteration(a=2, prep=2, prep_b=b + 1, post=2, post_b=b - 1)
        iteration(a=2, post=2, post_b=B - 2)
        iteration(post=2, post_b=B - 1)
        att.close()

        moe = ExitStack()
        W1 = sb("W1", [P, E, F], F32, moe)
        W2 = sb("W2", [P, E, F // P, C], F32, moe)
        FB = sb("FB", [P, E, F // P], F32, moe)
        GW = sb("GW", [P, E], F32, moe)
        GB = sb("GB", [P, E], F32, moe)
        B2R = sb("B2R", [E, C], F32, moe)
        iota = sb("iota", [P, E], F32, moe)
        LG = sb("LG", [P, NT, E], F32, moe)
        top = sb("top", [P, NT, 8], F32, moe)
        pos = sb("pos", [P, NT, 8], U32, moe)
        posf = sb("posf", [P, NT, 8], F32, moe)
        OH = sb("OH", [P, NT, E], F32, moe)
        OHT = sb("OHT", [E, T], F32, moe)
        MID = sb("MID", [P, 2, F // P, HALF], F32, moe)
        YM = sb("YM", [P, 2, HALF // P, C], F32, moe)
        ACC = sb("ACC", [P, NT, C], F32, moe)
        pT = moe.enter_context(nc.psum_tensor("pT", [P, T], F32))
        pH = moe.enter_context(nc.psum_tensor("pH", [P, 4, HALF], F32))
        pY = moe.enter_context(nc.psum_tensor("pY", [P, 2, HALF], F32))
        NF = F // P
        w_loads = [(W1[:], w1.rearrange("e c f -> c e f")), (W2[:], w2.rearrange("e (f p) c -> p (e f) c", p=P)
                   .rearrange("p (e f) c -> p e f c", e=E)), (FB[:], b1.rearrange("e (f p) -> p e f", p=P)),
                   (GW[:], gate_w), (GB[:], gate_b.rearrange("(o e) -> o e", o=1).to_broadcast([P, E])),
                   (B2R[:], b2), (iota[:], iota_e)]

        with nc.Block() as block:
            @block.sync
            def _(sp):
                with nc.allow_non_contiguous_dma(reason="one column per bias"):
                    for dst, src in w_loads:
                        sp.dma_start(dst, src).then_inc(w_in, 16)
                sp.wait_ge(w_in, 16 * len(w_loads))
        end_iteration()

        def experts(b):
            runs = [(c, e) for c in range(T // HALF) for e in range(E)]
            with nc.Block() as block:
                @block.sync
                def _(sp):
                    sp.dma_start(XIN[:], xa_d[b]).then_inc(xin_in, 16)
                    sp.dma_start(RES[:], x1_d[b]).then_inc(res_in, 16)
                    sp.wait_ge(res_done, 1)
                    sp.dma_start(out_t[b], RES[:]).then_inc(out_done, 16)
                    sp.wait_ge(out_done, 16)

                @block.vector
                def _(dve):
                    links = [0]

                    def link(ins):
                        links[0] += 1
                        ins.then_inc(dve_chain, 1)
                        dve.wait_ge(dve_chain, links[0])

                    def norm(src, dst, nth):
                        for t in range(NT):
                            last = nc.vector.bn_stats(st6[:, t, :], src[:, t, :])
                        link(last)
                        for t in range(NT):
                            last = nc.vector.bn_aggr(mv[:, t, :], st6[:, t, :])
                        last.then_inc(stats_done, 1)
                        dve.wait_ge(rstd_done, nth)
                        for t in range(NT):
                            last = nc.vector.tensor_scalar(dst[:, t, :], src[:, t, :], mv[:, t, 0:1],
                                                           rstd[:, t:t + 1], ALU.subtract, ALU.mult)
                        last.then_inc(norm_done, 1)

                    dve.wait_ge(xin_in, 16)
                    norm(XIN, XH, 1)
                    dve.wait_ge(slot_full[0], 2)
                    link(nc.vector.tensor_tensor(LG[:], pT[:, 0:NT * E].rearrange("p (t e) -> p t e", t=NT),
                                                 GB[:].unsqueeze(1).to_broadcast([P, NT, E]), ALU.add))
                    for t in range(NT):
                        last = nc.vector.max(top[:, t, :], LG[:, t, :])
                    link(last)
                    for t in range(NT):
                        last = nc.vector.max_index(pos[:, t, :], top[:, t, :], LG[:, t, :])
                    link(last)
                    link(nc.vector.tensor_copy(posf[:], pos[:]))
                    nc.vector.tensor_tensor(OH[:], posf[:, :, 0:1].to_broadcast([P, NT, E]),
                                            iota[:].unsqueeze(1).to_broadcast([P, NT, E]), ALU.is_equal)\
                        .then_inc(routed, 1)
                    dve.wait_ge(slot_full[0], 4)
                    link(nc.vector.tensor_tensor(ACC[:], XIN[:], pT[:].rearrange("p (t c) -> p t c", t=NT), ALU.add))
                    nc.vector.drain().then_inc(slot_free[0], 1)
                    for n, (c, e) in enumerate(runs):
                        dve.wait_ge(y_full, n + 1)
                        if n >= 2:
                            dve.wait_ge(y_added, n - 1)
                        q = HALF // P
                        nc.vector.tensor_tensor(YM[:, n % 2], pY[:, n % 2, :].rearrange("p (t c) -> p t c", t=q),
                                                OH[:, c * q:(c + 1) * q, e:e + 1].to_broadcast([P, q, C]), ALU.mult)\
                            .then_inc(y_used, 1)
                    dve.wait_ge(y_added, len(runs))
                    norm(ACC, ACC, 2)

                @block.gpsimd
                def _(pool):
                    def inverse(nth):
                        pool.wait_ge(stats_done, nth)
                        nc.gpsimd.tensor_scalar(rstd[:], mv[:, :, 1], EPS, None, ALU.add).then_inc(pool_chain, 1)
                        pool.wait_ge(pool_chain, nth)
                        nc.gpsimd.tensor_tensor(rstd[:], rstd[:], halfneg[:], ALU.pow).then_inc(rstd_done, 1)

                    inverse(1)
                    pool.wait_ge(slot_free[0], 1)
                    for n, (c, e) in enumerate(runs):
                        q = HALF // P
                        pool.wait_ge(y_used, n + 1)
                        if n:
                            pool.wait_ge(y_added, n)
                        nc.gpsimd.tensor_tensor(ACC[:, c * q:(c + 1) * q, :], ACC[:, c * q:(c + 1) * q, :],
                                                YM[:, n % 2], ALU.add).then_inc(y_added, 1)
                    inverse(2)
                    pool.wait_ge(norm_done, 2)
                    pool.wait_ge(res_in, 16)
                    nc.gpsimd.tensor_tensor(RES[:], RES[:], ACC[:], ALU.add).then_inc(res_done, 1)

                @block.scalar
                def _(act):
                    act.wait_ge(slot_full[0], 1)
                    nc.scalar.activation(XT[:], pT[:], ACT.Identity, bias=col[:, B2:B2 + 1],
                                         scale=col[:, G2:G2 + 1]).then_inc(slot_full[1], 1)
                    act.wait_ge(slot_full[0], 3)
                    nc.scalar.copy(OHT[:], pT[0:E, :]).then_inc(route_sb, 1)
                    for n, (c, e) in enumerate(runs):
                        for f in range(NF):
                            m = n * NF + f
                            act.wait_ge(h_full, m + 1)
                            if f == 0 and n >= 2:
                                act.wait_ge(y_full, n - 1)
                            nc.scalar.activation(MID[:, n % 2, f, :], pH[:, m % 4, :], ACT.Relu,
                                                 bias=FB[:, e, f:f + 1]).then_inc(h_done, 1)

                @block.tensor
                def _(pe):
                    pe.wait_ge(norm_done, 1)
                    for t in range(NT):
                        last = nc.tensor.transpose(pT[:, t * P:(t + 1) * P], XH[:, t, :], idf[:])
                    last.then_inc(slot_full[0], 1)
                    pe.wait_ge(slot_full[1], 1)
                    for t in range(NT):
                        last = nc.tensor.matmul(pT[:, t * E:(t + 1) * E], XT[:, t * P:(t + 1) * P], GW[:],
                                                start=True, stop=True)
                    last.then_inc(slot_full[0], 1)

                    def hidden(n):
                        c, e = runs[n]
                        for f in range(NF):
                            m = n * NF + f
                            if m >= 4:
                                pe.wait_ge(h_done, m - 3)
                            nc.tensor.matmul(pH[:, m % 4, :], W1[:, e, f * P:(f + 1) * P],
                                             XT[:, c * HALF:(c + 1) * HALF], start=True, stop=True).then_inc(h_full, 1)

                    def back(n):
                        c, e = runs[n]
                        pe.wait_ge(h_done, NF * (n + 1))
                        if n >= 2:
                            pe.wait_ge(y_used, n - 1)
                        for t in range(HALF // P):
                            for f in range(NF):
                                last = nc.tensor.matmul(pY[:, n % 2, t * C:(t + 1) * C],
                                                        MID[:, n % 2, f, t * P:(t + 1) * P], W2[:, e, f, :],
                                                        start=(f == 0), stop=(f == NF - 1))
                        last.then_inc(y_full, 1)

                    hidden(0)
                    pe.wait_ge(routed, 1)
                    for t in range(NT):
                        last = nc.tensor.transpose(pT[0:E, t * P:(t + 1) * P], OH[:, t, :], idf[:])
                    last.then_inc(slot_full[0], 1)
                    pe.wait_ge(route_sb, 1)
                    for t in range(NT):
                        last = nc.tensor.matmul(pT[:, t * C:(t + 1) * C], OHT[:, t * P:(t + 1) * P], B2R[:],
                                                start=True, stop=True)
                    last.then_inc(slot_full[0], 1)
                    for n in range(1, len(runs)):
                        hidden(n)
                        back(n - 1)
                    back(len(runs) - 1)
            end_iteration()

        with nc.Fori(0, B) as b:
            experts(b)
        moe.close()


def kernel(L0_attn_x, L0_attn_W_qkv, L0_attn_b_qkv, L0_attn_W_proj, L0_attn_b_proj, L0_ffn_ln1_g, L0_ffn_ln1_b,
           L0_ffn_ln2_g, L0_ffn_ln2_b, L0_ffn_wq, L0_ffn_bq, L0_ffn_wk, L0_ffn_bk, L0_ffn_wv, L0_ffn_bv, L0_ffn_wo,
           L0_ffn_bo, L0_ffn_gate_w, L0_ffn_gate_b, L0_ffn_w1, L0_ffn_b1, L0_ffn_w2, L0_ffn_b2):
    import concourse.bacc as bacc
    from concourse.bass_utils import run_bass_kernel_spmd
    import ml_dtypes

    ch = np.arange(C)
    by_d = (ch % H) * D + ch // H
    partner = (ch % H) * D + (ch // H) // 2 * 2 + (1 - (ch // H) % 2)
    W, bb = np.asarray(L0_attn_W_qkv), np.asarray(L0_attn_b_qkv)
    d = ch // H
    freqs = (10000.0 ** (-2.0 * np.arange(D // 2) / D)).astype(np.float32)
    angles = (np.arange(T, dtype=np.float32)[None, :] * freqs[d // 2][:, None]).astype(np.float32).astype(np.float64)
    sign = np.where(d % 2 == 0, -1.0, 1.0)[:, None]
    tri = np.arange(P)
    bf16 = ml_dtypes.bfloat16
    data = {
        "x": L0_attn_x, "wqs": W[:, 0:C][:, partner], "wks": W[:, C:2 * C][:, partner],
        "wq1": W[:, 0:C][:, by_d], "wk1": W[:, C:2 * C][:, by_d], "wv1": W[:, 2 * C:],
        "bq1": bb[0:C][by_d], "bqs": bb[0:C][partner], "bk1": bb[C:2 * C][by_d], "bks": bb[C:2 * C][partner],
        "bv1": bb[2 * C:], "wp1": L0_attn_W_proj, "bp1": L0_attn_b_proj,
        "ln1g": L0_ffn_ln1_g, "ln1b": L0_ffn_ln1_b, "ln2g": L0_ffn_ln2_g, "ln2b": L0_ffn_ln2_b,
        "wq2": np.asarray(L0_ffn_wq)[:, by_d], "wk2": np.asarray(L0_ffn_wk)[:, by_d], "wv2": L0_ffn_wv,
        "bq2": np.asarray(L0_ffn_bq)[by_d], "bk2": np.asarray(L0_ffn_bk)[by_d], "bv2": L0_ffn_bv,
        "wo2": L0_ffn_wo, "bo2": L0_ffn_bo, "gate_w": L0_ffn_gate_w, "gate_b": L0_ffn_gate_b,
        "w1": L0_ffn_w1, "b1": L0_ffn_b1, "w2": L0_ffn_w2, "b2": L0_ffn_b2,
        "cos": np.cos(angles).astype(np.float32), "sin": (sign * np.sin(angles)).astype(np.float32),
        "ident": np.eye(P, dtype=np.float32),
        "causal_q": np.where(tri[None, :] > tri[:, None], NEG, 0.0).astype(bf16),
        "causal_k": np.where(tri[:, None] > tri[None, :], NEG, 0.0).astype(bf16),
        "iota_e": np.tile(np.arange(E, dtype=np.float32), (P, 1)),
    }
    nc = bacc.Bacc("TRN2", target_bir_lowering=False, num_devices=1)
    arrays, aps = {}, {}
    for name, v in data.items():
        v = np.ascontiguousarray(v)
        arrays[f"in_{name}"] = v
        aps[name] = nc.dram_tensor(f"in_{name}", v.shape, mybir.dt.from_np(v.dtype), kind="ExternalInput").ap()
    out = nc.dram_tensor("out_dram", (B, T, C), F32, kind="ExternalOutput").ap()
    build_kernel(nc, out=out, **aps)
    r = run_bass_kernel_spmd(nc, [arrays], core_ids=[0])
    return r.results[0]["out_dram"]
```

```python
from contextlib import ExitStack

import numpy as np

import concourse.bass as bass
from concourse import mybir

F32 = mybir.dt.float32
BF16 = mybir.dt.bfloat16
U32 = mybir.dt.uint32
I32 = mybir.dt.int32
ALU = mybir.AluOpType
ACT = mybir.ActivationFunctionType
AX = mybir.AxisListType

P = 128
B, T, C = 4, 1024, 128
H, D = 16, 8
E, F = 8, 512
NT = T // P
G = 4
HG = H // G
HALF = 512
NPART = 3
STACK = NPART * NPART * D
MROW = 96
KROWS = MROW + NPART
Q_OUT = 16 * NPART * 2
SLOTS = 40
PER = 8
DEEP = 4
STACK_IN = 16 * (1 + NPART)
SCALE = float(D) ** -0.5
EPS = 1e-5
NEG = -3.0e38


def attend_steps(causal):
    out = []
    for half in range(T // HALF):
        for kt in range(NT):
            if causal and kt * P >= (half + 1) * HALF:
                continue
            off = max(0, kt * P - half * HALF) if causal else 0
            out.append((half, kt, off, causal and kt * P >= half * HALF))
    return out


def max_units(causal):
    return [(j, qt, P * (qt + 1) if causal else T) for half in range(2) for j in range(HG)
            for qt in range(half * NT // 2, (half + 1) * NT // 2)]


SLOTTED = ("max", "turn", "side")


def plan(a, prep, post):
    before_q = ["stats n1", "norm n1"] + (["stats n2", "norm n2"] if prep == 2 else [])
    side = {}
    if post:
        side[0, 0] = [("rec",), ("out", "rec")]
        side[0, 4] = [("at",)]
        side[0, 5] = [("side", "proj")] + ([("stats", "post")] if post == 1 else [])
        side[0, 7] = ([("norm", "post")] if post == 1 else []) + [("add",)]
        side[0, 9] = [("out", "res")]
        if post == 2:
            side[0, 8] = [("stats", "moe")]
            side[0, 9] += [("norm", "moe")]
            side[0, 11] = [("side", "ht"), ("hn",)]
            side[1, 8] = [("side", "lg"), ("out", "hn")]
    if prep:
        for n, what in enumerate(before_q):
            key = divmod((8 if post == 1 or prep == 1 else 12) + n, len(attend_steps(a == 1)))
            side[key] = side.get(key, []) + [tuple(what.split())]
        cuts = ["sum"] * (prep == 1) + ["0", "1", "2", "3"]
        side[1, 1] = side.get((1, 1), []) + [("side", "xt")]
        side[1, 2] = side.get((1, 2), []) + [("side", "q")]
        side[1, 3] = [("side", "qs")] if prep == 1 else [("out", "xn")]
        side[2, 2] = [("out", "q")]
        side[2, 4] = [("side", "k")]
        side[2, 5] = [("side", "ks")] if prep == 1 else []
        side[1, 6] = [("side", "v")]
        for n, what in enumerate(cuts):
            for name, key in (("q", (1, 4 + n + n // 2)), ("k", (2, 6 + n))):
                side[key] = side.get(key, []) + [("cut", name, what)]
        side[2, 11] = side.get((2, 11), []) + [("out", "k"), ("load", 0)]
        side[3, 3] = [("vg", 0), ("vg", 1), ("vg", 2), ("load", 1)]
        side[3, 5] = [("load", 2)]
    if a is None:
        items = [it for key in sorted(side) for it in side[key]]
        if prep:
            items += max_items(0, prep == 1)
        return [(None, [it]) for it in items]
    causal = a == 1
    side[0, 0] = [("load", G - 1), ("vg", G - 1)] + side.get((0, 0), [])
    side[0, 3] = side.get((0, 3), [])
    for g in range(G):
        side[g, 1] = [("turn", 1, g)] + side.get((g, 1), [])
        if g:
            side[g, 3] = side.get((g, 3), []) + [("heads", g - 1)]
    steps = attend_steps(causal)
    pace = np.cumsum([HALF - off + 150 for _, _, off, _ in steps])
    ticks = []
    for g in range(G):
        todo = [side.get((g, s), []) for s in range(len(steps))]
        if prep or g < G - 1:
            causal_next = causal if g < G - 1 else prep == 1
            units = max_items((g + 1) % G, causal_next)
            cost = np.cumsum([0.0] + [keys + 100 for _, _, keys in max_units(causal_next)])
            s = 0
            for it in units:
                if it[0] == "max":
                    s = int(np.searchsorted(pace / pace[-1], (cost[it[2]] + cost[it[2] + 1]) / 2 / cost[-1]))
                todo[s] = todo[s] + [it]
        for s, (half, kt, off, diag) in enumerate(steps):
            last_kt = max(k for h, k, _, _ in steps if h == half)
            ticks.append(((g, half, kt, off, diag, last_kt, 2 * g + half), todo[s]))
    return ticks


def max_items(g, causal):
    items = []
    for u in range(HG * NT):
        items.append(("max", g, u, causal))
        if u % 16 == 15:
            items.append(("split", u // 16, g, items[-1]))
        if u == 19:
            items.append(("turn", 0, g))
    return items


def build_kernel(nc, x, wqs, wks, wq1, wk1, wv1, bq1, bqs, bk1, bks, bv1, wp1, bp1,
                 ln1g, ln1b, ln2g, ln2b, wq2, wk2, wv2, bq2, bk2, bv2, wo2, bo2,
                 gate_w, gate_b, w1, b1, w2, b2, cos, sin, key_rows, ident, causal_q, causal_k, counting, zeros, before, out):
    x_t = x.rearrange("b (t p) c -> b p t c", p=P)
    out_t = out.rearrange("b (t p) c -> b p t c", p=P)

    def scratch(name, shape, dt):
        return nc.dram_tensor(name, shape, dt, kind="Internal").ap()

    q_d = scratch("q_scratch", [NPART, D, G, 2 * HG * HALF], BF16)
    k_d = scratch("k_scratch", [NPART, P, T], BF16)
    heads_d = scratch("heads_scratch", [G, P, T], F32)
    hn_d = scratch("hn_scratch", [B, P, NT, C], F32)
    sorted_d = scratch("sorted_scratch", [SLOTS * P, C], F32)
    result_d = scratch("result_scratch", [SLOTS * P, C], F32)
    rec_d = scratch("rec_scratch", [H, T], F32)
    x1_d = scratch("x1_scratch", [B, P, NT, C], F32)
    xn_d = scratch("xn_scratch", [B, P, NT, C], F32)
    xa_d = scratch("xa_scratch", [B, P, NT, C], F32)

    with ExitStack() as whole:
        def sem(name, ctx=whole):
            return ctx.enter_context(nc.semaphore(name))

        def sb(name, shape, dt=F32, ctx=whole):
            return ctx.enter_context(nc.sbuf_tensor(name, shape, dt))

        idf = sb("idf", [P, P])
        wgt = {n: sb(f"w_{n}", [P, C]) for n in ("q1", "qs1", "k1", "ks1", "v1", "o1", "q2", "k2", "v2", "o2")}
        col = sb("col", [P, 10])
        rows = sb("rows", [P, 6, C])
        XT = sb("XT", [P, T])
        XIN = sb("XIN", [P, NT, C])
        XH = sb("XH", [P, NT, C])
        XH2 = sb("XH2", [P, NT, C])
        Y = sb("Y", [P, NT, C])
        RES = sb("RES", [P, NT, C])
        st6 = sb("st6", [P, NT, 6])
        mv = sb("mv", [P, NT, 2])
        rstd = sb("rstd", [P, NT])
        halfneg = sb("halfneg", [P, NT])
        GW = sb("GW", [P, E])
        GB = sb("GB", [P, E])
        iota = sb("iota", [P, SLOTS])
        LG = sb("LG", [P, NT, E])
        top = sb("top", [P, NT, 8])
        pos8 = sb("pos8", [P, NT, 8], U32)
        pos8f = sb("pos8f", [P, NT, 8])
        OHB = sb("OHB", [P, NT, E])
        OH = sb("OH", [P, B, NT * E])
        BQ1, BQS, BK1, BKS, BQ2, BK2, G1, B1, G2, B2 = range(10)

        s_load = sem("s_load")
        s_init = sem("s_init")
        s_before, s_hn, s_sorted, w_in, counted, placed = (
            sem(n) for n in ("s_before", "s_hn", "s_sorted", "w_in", "counted", "placed"))
        mo_in = [sem(f"mo_in{b}") for b in range(B)]
        xa_in = [sem(f"xa_in{b}") for b in range(B)]
        s_zero = sem("s_zero")
        s_zeroed = sem("s_zeroed")

        iteration_sems = []

        def isem(name):
            iteration_sems.append(sem(name))
            return iteration_sems[-1]

        slot_full = [isem(f"slot_full{n}") for n in range(2)]
        slot_free = [isem(f"slot_free{n}") for n in range(2)]
        st_full = isem("st_full")
        exp_done = isem("exp_done")
        av_done = isem("av_done")
        o_evacuated = isem("o_evacuated")
        max_split = isem("max_split")
        rows_in = [isem(f"rows_in{n}") for n in range(2)]
        xin_in, res_in, xn_out, res_out = isem("xin_in"), isem("res_in"), isem("xn_out"), isem("res_out")
        stats_done, rstd_done, norm_done = isem("stats_done"), isem("rstd_done"), isem("norm_done")
        split_done, parts_out = isem("split_done"), isem("parts_out")
        vg_done = isem("vg_done")
        stack_in = [isem(f"stack_in{g}") for g in range(G)]
        heads_in = [isem(f"heads_in{n}") for n in range(2)]
        hn_done, hn_out = isem("hn_done"), isem("hn_out")
        den_in, num_in = isem("den_in"), isem("num_in")
        rec_out, rec_in = isem("rec_out"), isem("rec_in")
        rec_done, at_done, res_done = isem("rec_done"), isem("at_done"), isem("res_done")
        pool_chain, dve_chain = isem("pool_chain"), isem("dve_chain")
        h_full, h_done, y_full, y_used, x_turned, xts_done, fetched, out_done = (
            sem(n) for n in ("h_full", "h_done", "y_full", "y_used", "x_turned", "xts_done", "fetched", "out_done"))
        xs_in = [sem(f"xs_in{n}") for n in range(PER)]
        ys_out = [sem(f"ys_out{n}") for n in range(PER)]

        def end_iteration():
            nc.all_engine_barrier(sems_to_clear=range(iteration_sems[0].num, iteration_sems[-1].num + 1))

        loads = [(idf[:], ident), (wgt["o1"][:], wp1), (wgt["o2"][:], wo2),
                 (wgt["q1"][:], wq1), (wgt["qs1"][:], wqs), (wgt["k1"][:], wk1), (wgt["ks1"][:], wks),
                 (wgt["v1"][:], wv1), (wgt["q2"][:], wq2), (wgt["k2"][:], wk2), (wgt["v2"][:], wv2)]
        for n, v in enumerate((bq1, bqs, bk1, bks, bq2, bk2, ln1g, ln1b, ln2g, ln2b)):
            loads.append((col[:, n:n + 1], v.rearrange("(c o) -> c o", o=1)))
        for n, v in enumerate((bv1, bp1, bv2, bo2, ln2g, ln2b)):
            loads.append((rows[:, n, :], v.rearrange("(o c) -> o c", o=1).to_broadcast([P, C])))

        loads += [(GW[:], gate_w), (GB[:], gate_b.rearrange("(o e) -> o e", o=1).to_broadcast([P, E])),
                  (iota[:], counting)]

        att = ExitStack()
        QS = [sb(f"QS{g}", [KROWS, 2, HG, HALF], BF16, att) for g in range(G)]
        KS = [sb(f"KS{g}", [KROWS, HG, T], BF16, att) for g in range(G)]
        VG = [sb(f"VG{g}", [P, NT, HG, 32], F32, att) for g in range(G)]
        PT = sb("PT", [P, 2, HG, HALF], F32, att)
        OT = sb("OT", [P, 2, T], F32, att)
        NUM = sb("NUM", [P, T], F32, att)
        DEN = sb("DEN", [P, P], F32, att)
        REC = sb("REC", [P, T], F32, att)
        T1 = sb("T1", [P, T], F32, att)
        T2 = sb("T2", [P, T], F32, att)
        parts = sb("parts", [P, NPART, T], BF16, att)
        cos_sb = sb("cos_sb", [P, T], F32, att)
        sin_sb = sb("sin_sb", [P, T], F32, att)
        VST = sb("VST", [P, NT, C], F32, att)
        idb = sb("idb", [P, P], BF16, att)
        mask_q = sb("mask_q", [P, P], BF16, att)
        mask_k = sb("mask_k", [P, P], BF16, att)
        NM = sb("NM", [P, 2, 16], F32, att)
        NMR = sb("NMR", [P, 2, 16], F32, att)
        NMP = sb("NMP", [P, 2, NPART, 16], BF16, att)
        NMT = sb("NMT", [NPART * 16, 2, P], BF16, att)
        slots = [att.enter_context(nc.psum_tensor(f"slot{n}", [P, T], F32)) for n in range(2)]
        stb = att.enter_context(nc.psum_tensor("stb", [P, 3, HALF], F32))
        OB = att.enter_context(nc.psum_tensor("OB", [P, HALF], F32))
        AT = sb("AT", [P, T], F32, att)
        for g in range(G):
            loads += [(KS[g][STACK:KROWS].rearrange("p h t -> p (h t)"), key_rows),
                      (QS[g][STACK:MROW].rearrange("p s h t -> p (s h t)"), key_rows[0:MROW - STACK])]
        loads += [(cos_sb[:], cos), (sin_sb[:], sin), (mask_q[:], causal_q), (mask_k[:], causal_k)]

        with nc.Block() as block:
            @block.sync
            def _(sp):
                for dst, src in loads:
                    sp.dma_start(dst, src).then_inc(s_load, 16)
                sp.dma_start(sorted_d.rearrange("(s p) c -> s (p c)", p=P),
                             zeros.rearrange("p c -> (p c)").unsqueeze(0).to_broadcast([SLOTS, P * C]))\
                    .then_inc(s_zeroed, 16)
                sp.wait_ge(s_load, 16 * len(loads))

            @block.vector
            def _(dve):
                nc.vector.memset(halfneg[:], -0.5).then_inc(s_init, 1)
                dve.wait_ge(s_load, 16 * len(loads))
                nc.vector.tensor_copy(idb[:], idf[:]).then_inc(s_init, 1)

            @block.gpsimd
            def _(pool):
                for g in range(G):
                    nc.gpsimd.memset(VG[g][:, :, :, D:2 * D], 1.0)
                    nc.gpsimd.memset(VG[g][:, :, :, 2 * D:32], 0.0).then_inc(s_zero, 1)
        nc.all_engine_barrier()


        def iteration(a=None, prep=None, prep_b=None, post=None, post_b=None):
            ticks = plan(a, prep, post)
            order = [it for _, items in ticks for it in items if it[0] in SLOTTED]
            slot_use = {it: n for n, it in enumerate(order)}
            splits = [it for _, items in ticks for it in items if it[0] == "split"]
            turns = [it for it in order if it[0] == "turn"]
            n_steps = sum(step is not None for step, _ in ticks)
            per_group = n_steps // G

            def slot_of(it):
                return slot_use[it]

            def wait_slot_free(eng, it):
                n = slot_of(it)
                if n >= 2:
                    eng.wait_ge(slot_free[n % 2], n // 2)

            def wait_slot_full(eng, it):
                n = slot_of(it)
                eng.wait_ge(slot_full[n % 2], n // 2 + 1)

            def wait_slot_emptied(eng, it):
                n = slot_of(it)
                eng.wait_ge(slot_free[n % 2], n // 2 + 1)

            def emptied(ins, it):
                ins.then_inc(slot_free[slot_of(it) % 2], 1)

            def slot(it):
                return slots[slot_of(it) % 2]

            norms = [it[1] for _, items in ticks for it in items if it[0] == "stats"]
            norm_src = {"post": Y, "moe": RES, "n1": XIN, "n2": XH}
            norm_dst = {"post": Y, "moe": Y, "n1": XH, "n2": XH2}

            def units(it):
                return max_units(it[3])[it[2]]

            with nc.Block() as block:
                @block.sync
                def _(sp):
                    ends = {}

                    def load_stack(g):
                        kv = k_d.rearrange("j (d h) t -> (j d) h t", d=D)[:, HG * g:HG * (g + 1), :]
                        kv = kv.rearrange("r h t -> r (h t)").unsqueeze(0).to_broadcast([NPART, NPART * D, HG * T])
                        sp.dma_start(KS[g][0:STACK].rearrange("r h t -> r (h t)"), kv).then_inc(stack_in[g], 16)
                        for i in range(NPART):
                            qv = q_d[i, :, g].unsqueeze(0).to_broadcast([NPART, D, HG * T])
                            sp.dma_start(QS[g][i * NPART * D:(i + 1) * NPART * D].rearrange("r s h t -> r (s h t)"), qv)\
                                .then_inc(stack_in[g], 16)
                        ends[stack_in[g]] = STACK_IN

                    def heads_out(g):
                        if g < G - 1:
                            sp.wait_ge(o_evacuated, 2 * (g + 1))
                        if g == 0 and post:
                            sp.wait_ge(den_in, 16)
                            sp.wait_ge(num_in, 16)
                        sp.dma_start(heads_d[g], OT[:, g % 2, :]).then_inc(heads_in[g % 2], 16)
                        ends[heads_in[g % 2]] = ends.get(heads_in[g % 2], 0) + 16

                    if prep:
                        sp.dma_start(XIN[:], x_t[prep_b] if prep == 1 else x1_d[prep_b]).then_inc(xin_in, 16)
                    if post:
                        heads_out(G - 1)
                        sp.wait_ge(heads_in[1], 16)
                        hv = heads_d.rearrange("g (j r) t -> (g j) r t", j=HG)
                        sp.dma_start(DEN[:], hv[:, D, :].rearrange("h (t q) -> h t q", q=P)).then_inc(den_in, 16)
                        sp.dma_start(NUM[:], hv[:, 0:D, :]).then_inc(num_in, 16)
                        sp.dma_start(RES[:], x_t[post_b] if post == 1 else xn_d[post_b]).then_inc(res_in, 16)
                    for _, items in ticks:
                        for it in items:
                            if it[0] == "turn":
                                _, half, g = it
                                wait_slot_emptied(sp, it)
                                sp.dma_start(QS[g][MROW:KROWS, half].rearrange("p h (t q) -> p (h t) q", q=P),
                                             NMT[:, half, :]).then_inc(rows_in[half], 16)
                                ends[rows_in[half]] = ends.get(rows_in[half], 0) + 16
                            elif it[0] == "load":
                                g = it[1]
                                if g < G - 1:
                                    sp.wait_ge(parts_out, Q_OUT + 16)
                                    if a:
                                        sp.wait_ge(av_done, per_group * (g + 1))
                                load_stack(g)
                            elif it[0] == "heads":
                                heads_out(it[1])
                            elif it == ("out", "rec"):
                                sp.wait_ge(rec_done, 1)
                                sp.dma_start(rec_d.rearrange("h (t q) -> (h t) q", q=P), DEN[:]).then_inc(rec_out, 16)
                                sp.wait_ge(rec_out, 16)
                                sp.dma_start(REC[:], rec_d.unsqueeze(1).to_broadcast([H, D, T])).then_inc(rec_in, 16)
                                ends[rec_in] = 16
                            elif it[0] == "out":
                                if it[1] == "res":
                                    sp.wait_ge(res_done, 1)
                                    sp.dma_start(x1_d[post_b] if post == 1 else xa_d[post_b], RES[:])\
                                        .then_inc(res_out, 16)
                                    ends[res_out] = 16
                                elif it[1] == "hn":
                                    sp.wait_ge(hn_done, 1)
                                    sp.dma_start(hn_d[post_b], Y[:]).then_inc(hn_out, 16)
                                    ends[hn_out] = 16
                                elif it[1] == "xn":
                                    sp.wait_ge(norm_done, norms.index("n1") + 1)
                                    sp.dma_start(xn_d[prep_b], XH[:]).then_inc(xn_out, 16)
                                    ends[xn_out] = 16
                                else:
                                    n = "qk".index(it[1])
                                    if it[1] == "q" and a:
                                        sp.wait_ge(stack_in[G - 1], STACK_IN)
                                    sp.wait_ge(split_done, n + 1)
                                    if n:
                                        sp.dma_start(k_d.rearrange("j p t -> p j t"), parts[:]).then_inc(parts_out, 16)
                                    else:
                                        for i in range(NPART):
                                            for half in range(2):
                                                dst = q_d[i].rearrange("d g (s h t) -> (d g) s h t", s=2, t=HALF)
                                                sp.dma_start(dst[:, half],
                                                             parts[:, i, half * HALF:(half + 1) * HALF])\
                                                    .then_inc(parts_out, 16)
                                    ends[parts_out] = Q_OUT + 16 * n
                    for s, n in ends.items():
                        sp.wait_ge(s, n)

                @block.tensor
                def _(pe):
                    def do_max(it):
                        j, qt, keys = units(it)
                        g, causal = it[1], it[3]
                        if g in (0, G - 1):
                            pe.wait_ge(stack_in[g], STACK_IN)
                        wait_slot_free(pe, it)
                        w = QS[g][0:MROW, qt // 4, j, qt % 4 * P:(qt % 4 + 1) * P]
                        at = qt * P if causal else T
                        if causal:
                            nc.tensor.matmul(slot(it)[:, at:at + P], w, KS[g][0:MROW, j, at:at + P],
                                             start=True, stop=False)
                            last = nc.tensor.matmul(slot(it)[:, at:at + P], idb[:], mask_q[:], start=False, stop=True)
                        for c in range(0, min(at, keys), HALF):
                            e = min(c + HALF, at)
                            last = nc.tensor.matmul(slot(it)[:, c:e], w, KS[g][0:MROW, j, c:e], start=True, stop=True)
                        last.then_inc(slot_full[slot_of(it) % 2], 1)

                    def do_turn(it):
                        half = it[1]
                        if (half, it[2]) != (1, 0) or a is None:
                            pe.wait_ge(max_split, [x[1:3] for x in splits].index((half, it[2])) + 1)
                        wait_slot_free(pe, it)
                        nc.tensor.transpose(slot(it)[0:NPART * 16, 0:P // 2].bitcast(BF16),
                                            NMP[:, half, :, :].rearrange("p a b -> p (a b)"), idb[:])\
                            .then_inc(slot_full[slot_of(it) % 2], 1)

                    def do_side(it):
                        name = it[1]
                        wait_slot_free(pe, it)
                        o = slot(it)
                        if name == "xt":
                            pe.wait_ge(norm_done, norms.index("n2" if prep == 2 else "n1") + 1)
                            src = XH2 if prep == 2 else XH
                            for t in range(NT):
                                last = nc.tensor.transpose(o[:, t * P:(t + 1) * P], src[:, t, :], idf[:])
                        elif name in ("q", "qs", "k", "ks"):
                            wait_slot_emptied(pe, ("side", "xt"))
                            for c in range(0, T, HALF):
                                last = nc.tensor.matmul(o[:, c:c + HALF], wgt[f"{name}{prep}"][:], XT[:, c:c + HALF],
                                                        start=True, stop=True)
                        elif name == "v":
                            wait_slot_emptied(pe, ("side", "xt"))
                            for t in range(NT):
                                last = nc.tensor.matmul(o[:, t * P:(t + 1) * P], XT[:, t * P:(t + 1) * P],
                                                        wgt[f"v{prep}"][:], start=True, stop=True)
                        elif name == "ht":
                            pe.wait_ge(norm_done, norms.index("moe") + 1)
                            for t in range(NT):
                                last = nc.tensor.transpose(o[:, t * P:(t + 1) * P], Y[:, t, :], idf[:])
                        elif name == "lg":
                            wait_slot_emptied(pe, ("side", "ht"))
                            for t in range(NT):
                                last = nc.tensor.matmul(o[:, t * E:(t + 1) * E], T2[:, t * P:(t + 1) * P], GW[:],
                                                        start=True, stop=True)
                        elif name == "proj":
                            pe.wait_ge(at_done, 1)
                            for t in range(NT):
                                last = nc.tensor.matmul(o[:, t * P:(t + 1) * P], AT[:, t * P:(t + 1) * P],
                                                        wgt[f"o{post}"][:], start=True, stop=True)
                        last.then_inc(slot_full[slot_of(it) % 2], 1)

                    def item(it):
                        {"max": do_max, "turn": do_turn, "side": do_side}[it[0]](it)

                    def weigh(step, n):
                        g, half, kt, off, _, last_kt, chunk = step
                        pe.wait_ge(exp_done, HG * (n + 1))
                        if kt == 0 and chunk >= 1:
                            pe.wait_ge(o_evacuated, chunk)
                        if chunk == 2 * (G - 1) and kt == 0:
                            pe.wait_ge(vg_done, 1)
                        for j in range(HG):
                            last = nc.tensor.matmul(OB[32 * j:32 * j + 32, off:HALF], VG[g][:, kt, j, :],
                                                    PT[:, n % 2, j, off:HALF], start=(kt == 0), stop=(kt == last_kt),
                                                    skip_group_check=True)
                        last.then_inc(av_done, 1)

                    before = None
                    n = 0
                    for step, items in ticks:
                        mine = [it for it in items if it[0] in SLOTTED]
                        if step is None:
                            for it in mine:
                                item(it)
                            continue
                        g, half, kt, off, diag, last_kt, chunk = step
                        if kt == 0:
                            if g + half:
                                pe.wait_ge(rows_in[half], 16 * (g + half))
                        for j in range(HG):
                            m = HG * n + j
                            if m >= 3:
                                pe.wait_ge(exp_done, m - 2)
                            o = stb[:, m % 3, :]
                            w = KS[g][:, j, kt * P:(kt + 1) * P]
                            if diag:
                                nc.tensor.matmul(o[:, off:off + P], w, QS[g][:, half, j, off:off + P], start=True, stop=False)
                                last = nc.tensor.matmul(o[:, off:off + P], idb[:], mask_k[:], start=False, stop=True)
                                if off + P < HALF:
                                    last = nc.tensor.matmul(o[:, off + P:HALF], w,
                                                            QS[g][:, half, j, off + P:HALF], start=True, stop=True)
                            else:
                                last = nc.tensor.matmul(o[:, off:HALF], w, QS[g][:, half, j, off:HALF],
                                                        start=True, stop=True)
                            last.then_inc(st_full, 1)
                            if j == 1 and mine:
                                item(mine[0])
                            if j == 2 and before is not None:
                                weigh(before, n - 1)
                        for it in mine[1:]:
                            item(it)
                        before = step
                        n += 1
                    if before is not None:
                        weigh(before, n - 1)

                @block.scalar
                def _(act):
                    def evacuate(chunk):
                        g, half = divmod(chunk, 2)
                        gone = sum(h % 2 == g % 2 for h in ([G - 1] if post else []) + list(range(g)))
                        if half == 0 and gone:
                            act.wait_ge(heads_in[g % 2], 16 * gone)
                        nc.scalar.copy(OT[:, g % 2, half * HALF:(half + 1) * HALF], OB[:]).then_inc(o_evacuated, 1)

                    n = 0
                    done = None
                    for step, items in ticks:
                        if step is not None:
                            g, half, kt, off, diag, last_kt, chunk = step
                            for j in range(HG):
                                m = HG * n + j
                                act.wait_ge(st_full, m + 1)
                                if j == 0 and n >= 2:
                                    act.wait_ge(av_done, n - 1)
                                nc.scalar.activation(PT[:, n % 2, j, off:HALF], stb[:, m % 3, off:HALF], ACT.Exp,
                                                     scale=SCALE).then_inc(exp_done, 1)
                            if done is not None:
                                act.wait_ge(av_done, n)
                                evacuate(done)
                                done = None
                            if kt == last_kt:
                                done = chunk
                            n += 1
                        for it in items:
                            if it[0] == "turn":
                                wait_slot_full(act, it)
                                before = sum(x[1] == it[1] for x in turns[:turns.index(it)])
                                if before:
                                    act.wait_ge(rows_in[it[1]], 16 * before)
                                emptied(nc.scalar.copy(NMT[:, it[1], :],
                                                       slot(it)[0:NPART * 16, 0:P // 2].bitcast(BF16)), it)
                            elif it == ("side", "ht"):
                                wait_slot_full(act, it)
                                emptied(nc.scalar.activation(T2[:], slot(it)[:], ACT.Identity,
                                                             bias=col[:, B2:B2 + 1], scale=col[:, G2:G2 + 1]), it)
                            elif it == ("side", "xt"):
                                wait_slot_full(act, it)
                                if prep == 1:
                                    emptied(nc.scalar.copy(XT[:], slot(it)[:]), it)
                                else:
                                    emptied(nc.scalar.activation(XT[:], slot(it)[:], ACT.Identity,
                                                                 bias=col[:, B1:B1 + 1], scale=col[:, G1:G1 + 1]), it)
                    if done is not None:
                        act.wait_ge(av_done, n)
                        evacuate(done)

                @block.vector
                def _(dve):
                    links = [0]

                    def link(ins):
                        links[0] += 1
                        ins.then_inc(dve_chain, 1)
                        dve.wait_ge(dve_chain, links[0])

                    for it in (it for _, items in ticks for it in items):
                        if it[0] == "max":
                            j, qt, keys = units(it)
                            half = it[2] // 16
                            if it[2] % 16 == 0:
                                before = [n for n, x in enumerate(splits) if x[1] == half
                                          and splits.index(next(y for y in splits if y[1:3] == (half, it[1]))) > n]
                                if before:
                                    dve.wait_ge(max_split, before[-1] + 1)
                            wait_slot_full(dve, it)
                            at = j * 4 + qt % 4
                            emptied(nc.vector.tensor_reduce(NM[:, half, at:at + 1], slot(it)[:, 0:keys], AX.X,
                                                            ALU.max, negate=True), it)
                        elif it[0] == "rec":
                            dve.wait_ge(den_in, 16)
                            nc.vector.reciprocal(DEN[:], DEN[:]).then_inc(rec_done, 1)
                        elif it == ("side", "proj"):
                            wait_slot_full(dve, it)
                            bias = rows[:, 1 if post == 1 else 3, :].unsqueeze(1).to_broadcast([P, NT, C])
                            emptied(nc.vector.tensor_tensor(Y[:], slot(it)[:].rearrange("p (t c) -> p t c", t=NT),
                                                            bias, ALU.add), it)
                        elif it[0] == "stats":
                            src = norm_src[it[1]]
                            if it[1] == "post":
                                wait_slot_emptied(dve, ("side", "proj"))
                            elif it[1] == "moe":
                                dve.wait_ge(res_done, 1)
                            elif it[1] == "n1":
                                dve.wait_ge(xin_in, 16)
                            else:
                                dve.wait_ge(norm_done, norms.index("n1") + 1)
                            for t in range(NT):
                                last = nc.vector.bn_stats(st6[:, t, :], src[:, t, :])
                            link(last)
                            for t in range(NT):
                                last = nc.vector.bn_aggr(mv[:, t, :], st6[:, t, :])
                            last.then_inc(stats_done, 1)
                        elif it[0] == "norm":
                            dve.wait_ge(rstd_done, norms.index(it[1]) + 1)
                            for t in range(NT):
                                last = nc.vector.tensor_scalar(norm_dst[it[1]][:, t, :], norm_src[it[1]][:, t, :],
                                                               mv[:, t, 0:1], rstd[:, t:t + 1],
                                                               ALU.subtract, ALU.mult)
                            last.then_inc(norm_done, 1)
                        elif it[0] == "side" and it[1] in ("q", "k", "qs", "ks"):
                            wait_slot_full(dve, it)
                            if it[1] == "k":
                                dve.wait_ge(split_done, 1)
                            c = {"q1": BQ1, "qs1": BQS, "k1": BK1, "ks1": BKS, "q2": BQ2, "k2": BK2}[f"{it[1]}{prep}"]
                            if prep == 1:
                                dst, table = (T2, sin_sb) if it[1][1:] else (T1, cos_sb)
                                emptied(nc.vector.scalar_tensor_tensor(dst[:], slot(it)[:], col[:, c:c + 1], table[:],
                                                                       ALU.add, ALU.mult), it)
                            else:
                                emptied(nc.vector.tensor_scalar(T1[:], slot(it)[:], col[:, c:c + 1], None, ALU.add), it)
                        elif it == ("side", "lg"):
                            wait_slot_full(dve, it)
                            emptied(nc.vector.tensor_tensor(LG[:], slot(it)[:, 0:NT * E]
                                                            .rearrange("p (t e) -> p t e", t=NT),
                                                            GB[:].unsqueeze(1).to_broadcast([P, NT, E]), ALU.add), it)
                            wait_slot_emptied(dve, it)
                            for t in range(NT):
                                last = nc.vector.max(top[:, t, :], LG[:, t, :])
                            link(last)
                            for t in range(NT):
                                last = nc.vector.max_index(pos8[:, t, :], top[:, t, :], LG[:, t, :])
                            link(last)
                            link(nc.vector.tensor_copy(pos8f[:], pos8[:]))
                            link(nc.vector.tensor_tensor(OHB[:], pos8f[:, :, 0:1].to_broadcast([P, NT, E]),
                                                         iota[:, 0:E].unsqueeze(1).to_broadcast([P, NT, E]),
                                                         ALU.is_equal))
                            link(nc.vector.tensor_copy(OH[:, post_b], OHB[:].rearrange("p t e -> p (t e)")))
                        elif it == ("side", "v"):
                            wait_slot_full(dve, it)
                            if a:
                                dve.wait_ge(vg_done, 1)
                            bias = rows[:, 0 if prep == 1 else 2, :].unsqueeze(1).to_broadcast([P, NT, C])
                            emptied(nc.vector.tensor_tensor(VST[:], slot(it)[:].rearrange("p (t c) -> p t c", t=NT),
                                                            bias, ALU.add), it)

                @block.gpsimd
                def _(pool):
                    links = [0]

                    def link(ins):
                        links[0] += 1
                        ins.then_inc(pool_chain, 1)
                        pool.wait_ge(pool_chain, links[0])

                    def rounded(dst, src):
                        return nc.gpsimd.tensor_scalar(dst, src, 1.0, 0.0, ALU.mult, ALU.add)

                    for it in (it for _, items in ticks for it in items):
                        if it[0] == "split":
                            _, half, g, last = it
                            wait_slot_emptied(pool, last)
                            before = [t for t in turns if t[1] == half and order.index(t) < order.index(last)]
                            if before:
                                wait_slot_full(pool, before[-1])
                            link(rounded(NMP[:, half, 0, :], NM[:, half, :]))
                            link(nc.gpsimd.tensor_tensor(NMR[:, half, :], NM[:, half, :], NMP[:, half, 0, :],
                                                         ALU.subtract))
                            link(rounded(NMP[:, half, 1, :], NMR[:, half, :]))
                            nc.gpsimd.tensor_tensor(NMP[:, half, 2, :], NMR[:, half, :], NMP[:, half, 1, :],
                                                    ALU.subtract).then_inc(max_split, 1)
                        elif it[0] == "vg":
                            g = it[1]
                            if g < G - 1:
                                wait_slot_emptied(pool, ("side", "v"))
                                if a:
                                    pool.wait_ge(av_done, per_group * (g + 1))
                            nc.gpsimd.tensor_copy(VG[g][:, :, :, 0:D],
                                                  VST[:, :, g * HG * D:(g + 1) * HG * D]
                                                  .rearrange("p t (j d) -> p t j d", d=D)).then_inc(vg_done, 1)
                        elif it[0] == "at":
                            pool.wait_ge(num_in, 16)
                            pool.wait_ge(rec_in, 16)
                            nc.gpsimd.tensor_tensor(AT[:], NUM[:], REC[:], ALU.mult).then_inc(at_done, 1)
                        elif it[0] == "hn":
                            wait_slot_full(pool, ("side", "ht"))
                            for n, op in ((4, ALU.mult), (5, ALU.add)):
                                ins = nc.gpsimd.tensor_tensor(Y[:], Y[:], rows[:, n, :].unsqueeze(1)
                                                              .to_broadcast([P, NT, C]), op)
                                if n == 4:
                                    link(ins)
                            ins.then_inc(hn_done, 1)
                        elif it[0] == "add":
                            pool.wait_ge(res_in, 16)
                            if post == 1:
                                pool.wait_ge(norm_done, norms.index("post") + 1)
                            else:
                                wait_slot_emptied(pool, ("side", "proj"))
                            nc.gpsimd.tensor_tensor(RES[:], RES[:], Y[:], ALU.add).then_inc(res_done, 1)
                        elif it[0] == "stats":
                            pool.wait_ge(stats_done, norms.index(it[1]) + 1)
                            link(nc.gpsimd.tensor_scalar(rstd[:], mv[:, :, 1], EPS, None, ALU.add))
                            nc.gpsimd.tensor_tensor(rstd[:], rstd[:], halfneg[:], ALU.pow).then_inc(rstd_done, 1)
                        elif it[0] == "cut":
                            _, name, piece = it
                            if piece == "sum":
                                wait_slot_emptied(pool, ("side", name))
                                wait_slot_emptied(pool, ("side", name + "s"))
                                link(nc.gpsimd.tensor_tensor(T1[:], T1[:], T2[:], ALU.add))
                            elif piece == "0":
                                if prep == 2:
                                    wait_slot_emptied(pool, ("side", name))
                                if name == "k":
                                    pool.wait_ge(parts_out, Q_OUT)
                                link(rounded(parts[:, 0, :], T1[:]))
                            elif piece == "1":
                                link(nc.gpsimd.tensor_tensor(T1[:], T1[:], parts[:, 0, :], ALU.subtract))
                            elif piece == "2":
                                link(rounded(parts[:, 1, :], T1[:]))
                            else:
                                nc.gpsimd.tensor_tensor(parts[:, 2, :], T1[:], parts[:, 1, :], ALU.subtract)\
                                    .then_inc(split_done, 1)
            end_iteration()

        iteration(prep=1, prep_b=0)
        iteration(a=1, prep=1, prep_b=1)
        with nc.Fori(1, B - 1) as b:
            iteration(a=1, prep=1, prep_b=b + 1, post=1, post_b=b - 1)
        iteration(a=1, prep=2, prep_b=0, post=1, post_b=B - 2)
        iteration(a=2, prep=2, prep_b=1, post=1, post_b=B - 1)
        with nc.Fori(1, B - 1) as b:
            iteration(a=2, prep=2, prep_b=b + 1, post=2, post_b=b - 1)
        iteration(a=2, post=2, post_b=B - 2)
        iteration(post=2, post_b=B - 1)
        att.close()

        moe = ExitStack()
        NF = F // P
        WIDE = F + F + C + NF
        W = sb("W", [P, E, WIDE], F32, moe)
        WS = sb("WS", [P, DEEP, WIDE], F32, moe)
        BF = sb("BF", [P, 2, P], F32, moe)
        HN = sb("HN", [P, B * NT, C], F32, moe)
        ones = sb("ones", [P, B * NT], F32, moe)
        cnt = sb("cnt", [P, B * NT, E], F32, moe)
        upto = sb("upto", [P, B * NT, E], F32, moe)
        place = sb("place", [P, B * NT, E], F32, moe)
        need = sb("need", [P, E], F32, moe)
        needi = sb("needi", [P, E], I32, moe)
        tiles = sb("tiles", [P, E], F32, moe)
        tiles_upto = sb("tiles_upto", [P, E], F32, moe)
        first = sb("first", [P, E], F32, moe)
        spot = sb("spot", [P, B * NT], F32, moe)
        spoti = sb("spoti", [P, B * NT], U32, moe)
        passed = sb("passed", [P, SLOTS, E - 1], F32, moe)
        owner = sb("owner", [P, SLOTS], F32, moe)
        owneri = sb("owneri", [P, SLOTS], I32, moe)
        pR = moe.enter_context(nc.psum_tensor("pR", [P, 2, HALF], F32))

        w_loads = [(W[:, :, 0:F], w1.rearrange("e c f -> c e f"))]
        w_loads += [(W[:, e, F:2 * F].rearrange("p (f c) -> p f c", f=NF), w2[e].rearrange("(p f) c -> p f c", f=NF))
                    for e in range(E)]
        w_loads += [(W[:, :, 2 * F:2 * F + C], b2.unsqueeze(0).to_broadcast([P, E, C]))]
        w_loads += [(W[:, e, 2 * F + C:WIDE], b1[e].rearrange("(p f) -> p f", f=NF)) for e in range(E)]

        with nc.Block() as block:
            @block.sync
            def _(sp):
                sp.dma_start(BF[:], before).then_inc(s_before, 16)
                for b in range(B):
                    sp.dma_start(HN[:, b * NT:(b + 1) * NT, :], hn_d[b]).then_inc(s_hn, 16)
                for dst, src in w_loads:
                    sp.dma_start(dst, src).then_inc(w_in, 16)
                sp.wait_ge(w_in, 16 * len(w_loads))

            @block.tensor
            def _(pe):
                pe.wait_ge(s_before, 16)
                for n in range(2):
                    nc.tensor.matmul(pR[:, n, 0:B * NT * E], BF[:, n, :], OH[:].rearrange("p b te -> p (b te)"),
                                     start=True, stop=True).then_inc(counted, 1)

            @block.vector
            def _(dve):
                links = [0]

                def link(ins):
                    links[0] += 1
                    ins.then_inc(dve_chain, 1)
                    dve.wait_ge(dve_chain, links[0])

                link(nc.vector.memset(ones[:], 1.0))
                dve.wait_ge(counted, 2)
                link(nc.vector.tensor_copy(cnt[:], pR[:, 1, 0:B * NT * E].rearrange("p (t e) -> p t e", e=E)))
                for e in range(E):
                    last = nc.vector.tensor_tensor_scan(upto[:, :, e], ones[:], cnt[:, :, e], 0.0, ALU.mult, ALU.add)
                link(last)
                link(nc.vector.tensor_scalar(needi[:], upto[:, B * NT - 1, :], float(P - 1), None, ALU.add))
                link(nc.vector.tensor_scalar(needi[:], needi[:], 7, None, ALU.arith_shift_right))
                link(nc.vector.tensor_copy(tiles[:], needi[:]))
                link(nc.vector.tensor_tensor_scan(tiles_upto[:], ones[:, 0:E], tiles[:], 0.0, ALU.mult, ALU.add))
                link(nc.vector.tensor_tensor(first[:], tiles_upto[:], tiles[:], ALU.subtract))
                link(nc.vector.tensor_tensor(place[:], upto[:], cnt[:], ALU.subtract))
                link(nc.vector.tensor_tensor(place[:], pR[:, 0, 0:B * NT * E].rearrange("p (t e) -> p t e", e=E),
                                             place[:], ALU.add))
                link(nc.vector.tensor_scalar(need[:], first[:], float(P), None, ALU.mult))
                link(nc.vector.tensor_tensor(place[:], place[:], need[:].unsqueeze(1).to_broadcast([P, B * NT, E]),
                                             ALU.add))
                link(nc.vector.tensor_tensor(place[:], place[:], OH[:].rearrange("p b (t e) -> p (b t) e", e=E),
                                             ALU.mult))
                link(nc.vector.tensor_reduce(spot[:], place[:], AX.X, ALU.add))
                nc.vector.tensor_copy(spoti[:], spot[:]).then_inc(placed, 1)
                link(nc.vector.tensor_tensor(passed[:], iota[:].unsqueeze(2).to_broadcast([P, SLOTS, E - 1]),
                                             first[:, 1:E].unsqueeze(1).to_broadcast([P, SLOTS, E - 1]), ALU.is_ge))
                link(nc.vector.tensor_reduce(owner[:], passed[:], AX.X, ALU.add))
                link(nc.vector.tensor_copy(owneri[:], owner[:]))

            @block.gpsimd
            def _(pool):
                pool.wait_ge(placed, 1)
                pool.wait_ge(s_hn, 16 * B)
                pool.wait_ge(s_zeroed, 16)
                for t in range(B * NT):
                    nc.gpsimd.indirect_dma_start(
                        out=sorted_d, out_offset=bass.IndirectOffsetOnAxis(ap=spoti[:, t:t + 1], axis=0),
                        in_=HN[:, t, :], in_offset=None).then_inc(s_sorted, 16)
                pool.wait_ge(s_sorted, 16 * B * NT)
        end_iteration()

        slot_mem = ExitStack()
        XS = sb("XS", [P, PER, C], F32, slot_mem)
        XTS = sb("XTS", [P, 2, P], F32, slot_mem)
        MID = sb("MID", [P, 2, F], F32, slot_mem)
        YS = sb("YS", [P, PER, C], F32, slot_mem)
        pX = slot_mem.enter_context(nc.psum_tensor("pX", [P, 2, HALF], F32))
        pH = slot_mem.enter_context(nc.psum_tensor("pH", [P, 2, HALF], F32))
        pY = slot_mem.enter_context(nc.psum_tensor("pY", [P, 2, HALF], F32))
        sorted_v = sorted_d.rearrange("(i s p) c -> i p s c", p=P, s=PER)
        result_v = result_d.rearrange("(i s p) c -> i p s c", p=P, s=PER)
        ROUNDS = SLOTS // PER

        with nc.Block() as block:
            @block.sync
            def _(sp):
                def load(i, u):
                    sp.dma_start(XS[:, u, :], sorted_v[i][:, u, :]).then_inc(xs_in[u], 16)

                def store(i, u):
                    sp.wait_ge(y_used, i * PER + u + 1)
                    sp.dma_start(result_v[i][:, u, :], YS[:, u, :]).then_inc(ys_out[u], 16)

                for u in range(PER):
                    load(0, u)
                with sp.Fori(0, ROUNDS - 1) as i:
                    for u in range(PER):
                        sp.wait_ge(x_turned, i * PER + u + 1)
                        load(i + 1, u)
                        store(i, u)
                for u in range(PER):
                    store(ROUNDS - 1, u)
                for u in range(PER):
                    sp.wait_ge(ys_out[u], 16 * ROUNDS)

            @block.vector
            def _(dve):
                def fetch(i, u, first, e):
                    if not (first and u < DEEP):
                        dve.wait_ge(y_used, i * PER + u - DEEP + 1)
                    nc.vector.tensor_copy(WS[:, u % DEEP, :], W[:, bass.ds(e, 1), :].rearrange("p o w -> p (o w)"))\
                        .then_inc(fetched, 1)

                def bias(i, u, first):
                    dve.wait_ge(y_full, i * PER + u + 1)
                    if not first:
                        dve.wait_ge(ys_out[u], i * 16)
                    nc.vector.tensor_tensor(YS[:, u, :], pY[:, u % 2, 0:C], WS[:, u % DEEP, 2 * F:2 * F + C],
                                            ALU.add).then_inc(y_used, 1)

                def step(i, first, second=False):
                    experts = [dve.value_load(owneri[0:1, bass.ds(i * PER + u, 1)], min_val=0, max_val=E - 1)
                               for u in range(PER)]
                    for u in range(PER):
                        fetch(i, u, first, experts[u])
                        late = u - (DEEP - 1)
                        if late >= 0:
                            bias(i, late, first)
                        elif not first:
                            bias(i - 1, late + PER, second)

                step(0, True)
                step(1, False, True)
                with dve.Fori(2, ROUNDS) as i:
                    step(i, False)
                for u in range(PER - DEEP + 1, PER):
                    bias(ROUNDS - 1, u, False)

            @block.scalar
            def _(act):
                def turned(i, u, first):
                    act.wait_ge(x_turned, i * PER + u + 1)
                    if not (first and u < 2):
                        act.wait_ge(h_full, i * PER + u - 1)
                    nc.scalar.copy(XTS[:, u % 2, :], pX[:, u % 2, 0:P]).then_inc(xts_done, 1)

                def relu(i, u, first):
                    act.wait_ge(h_full, i * PER + u + 1)
                    if not (first and u < 2):
                        act.wait_ge(y_full, i * PER + u - 1)
                    for f in range(NF):
                        at = 2 * F + C + f
                        last = nc.scalar.activation(MID[:, u % 2, f * P:(f + 1) * P],
                                                    pH[:, u % 2, f * P:(f + 1) * P], ACT.Relu,
                                                    bias=WS[:, u % DEEP, at:at + 1])
                    last.then_inc(h_done, 1)

                def step(i, first, second=False):
                    for u in range(PER):
                        turned(i, u, first)
                        if u:
                            relu(i, u - 1, first)
                        elif not first:
                            relu(i - 1, PER - 1, second)

                step(0, True)
                step(1, False, True)
                with act.Fori(2, ROUNDS) as i:
                    step(i, False)
                relu(ROUNDS - 1, PER - 1, False)

            @block.tensor
            def _(pe):
                def turn(i, u, first):
                    pe.wait_ge(xs_in[u], (i + 1) * 16)
                    if not (first and u < 2):
                        pe.wait_ge(xts_done, i * PER + u - 1)
                    nc.tensor.transpose(pX[:, u % 2, 0:P], XS[:, u, :], idf[:]).then_inc(x_turned, 1)

                def hidden(i, u, first):
                    pe.wait_ge(xts_done, i * PER + u + 1)
                    pe.wait_ge(fetched, i * PER + u + 1)
                    if not (first and u < 2):
                        pe.wait_ge(h_done, i * PER + u - 1)
                    for f in range(NF):
                        w_f = WS[:, u % DEEP, 0:F].rearrange("c (p f) -> c f p", f=NF)[:, f, :]
                        last = nc.tensor.matmul(pH[:, u % 2, f * P:(f + 1) * P], w_f, XTS[:, u % 2, :],
                                                start=True, stop=True)
                    last.then_inc(h_full, 1)

                def back(i, u, first):
                    pe.wait_ge(h_done, i * PER + u + 1)
                    if not (first and u < 2):
                        pe.wait_ge(y_used, i * PER + u - 1)
                    for f in range(NF):
                        last = nc.tensor.matmul(pY[:, u % 2, 0:C], MID[:, u % 2, f * P:(f + 1) * P],
                                                WS[:, u % DEEP, F + f * C:F + (f + 1) * C],
                                                start=(f == 0), stop=(f == NF - 1))
                    last.then_inc(y_full, 1)

                def step(i, first, second=False):
                    for u in range(PER):
                        turn(i, u, first)
                        for stage, late in ((hidden, u - 1), (back, u - 2)):
                            if late >= 0:
                                stage(i, late, first)
                            elif not first:
                                stage(i - 1, late + PER, second)

                step(0, True)
                step(1, False, True)
                with pe.Fori(2, ROUNDS) as i:
                    step(i, False)
                hidden(ROUNDS - 1, PER - 1, False)
                back(ROUNDS - 1, PER - 2, False)
                back(ROUNDS - 1, PER - 1, False)
        nc.all_engine_barrier()
        slot_mem.close()

        MO = [sb(f"MO{b}", [P, NT, C], F32, moe) for b in range(B)]
        XA = [sb(f"XA{b}", [P, NT, C], F32, moe) for b in range(B)]
        X1 = [sb(f"X1{b}", [P, NT, C], F32, moe) for b in range(B)]
        with nc.Block() as block:
            def inverse(pool, nth):
                pool.wait_ge(stats_done, nth)
                nc.gpsimd.tensor_scalar(rstd[:], mv[:, :, 1], EPS, None, ALU.add).then_inc(pool_chain, 1)
                pool.wait_ge(pool_chain, nth)
                nc.gpsimd.tensor_tensor(rstd[:], rstd[:], halfneg[:], ALU.pow).then_inc(rstd_done, 1)

            @block.sync
            def _(sp):
                for b in range(B):
                    sp.dma_start(XA[b][:], xa_d[b]).then_inc(xa_in[b], 16)
                    sp.dma_start(X1[b][:], x1_d[b]).then_inc(xa_in[b], 16)
                for b in range(B):
                    sp.wait_ge(res_done, b + 1)
                    sp.dma_start(out_t[b], X1[b][:]).then_inc(out_done, 16)
                sp.wait_ge(out_done, 16 * B)

            @block.gpsimd
            def _(pool):
                for b in range(B):
                    for t in range(NT):
                        nc.gpsimd.indirect_dma_start(
                            out=MO[b][:, t, :], out_offset=None, in_=result_d,
                            in_offset=bass.IndirectOffsetOnAxis(ap=spoti[:, b * NT + t:b * NT + t + 1], axis=0))\
                            .then_inc(mo_in[b], 16)
                    if b:
                        inverse(pool, b)
                inverse(pool, B)

            @block.vector
            def _(dve):
                links = [0]

                def link(ins):
                    links[0] += 1
                    ins.then_inc(dve_chain, 1)
                    dve.wait_ge(dve_chain, links[0])

                for b in range(B):
                    dve.wait_ge(xa_in[b], 32)
                    dve.wait_ge(mo_in[b], 16 * NT)
                    link(nc.vector.tensor_tensor(MO[b][:], MO[b][:], XA[b][:], ALU.add))
                    for t in range(NT):
                        last = nc.vector.bn_stats(st6[:, t, :], MO[b][:, t, :])
                    link(last)
                    for t in range(NT):
                        last = nc.vector.bn_aggr(mv[:, t, :], st6[:, t, :])
                    last.then_inc(stats_done, 1)
                    dve.wait_ge(rstd_done, b + 1)
                    for t in range(NT):
                        last = nc.vector.tensor_scalar(MO[b][:, t, :], MO[b][:, t, :], mv[:, t, 0:1],
                                                       rstd[:, t:t + 1], ALU.subtract, ALU.mult)
                    link(last)
                    nc.vector.tensor_tensor(X1[b][:], X1[b][:], MO[b][:], ALU.add).then_inc(res_done, 1)
        moe.close()


def kernel(L0_attn_x, L0_attn_W_qkv, L0_attn_b_qkv, L0_attn_W_proj, L0_attn_b_proj, L0_ffn_ln1_g, L0_ffn_ln1_b,
           L0_ffn_ln2_g, L0_ffn_ln2_b, L0_ffn_wq, L0_ffn_bq, L0_ffn_wk, L0_ffn_bk, L0_ffn_wv, L0_ffn_bv, L0_ffn_wo,
           L0_ffn_bo, L0_ffn_gate_w, L0_ffn_gate_b, L0_ffn_w1, L0_ffn_b1, L0_ffn_w2, L0_ffn_b2):
    import concourse.bacc as bacc
    from concourse.bass_utils import run_bass_kernel_spmd
    import ml_dtypes

    ch = np.arange(C)
    by_d = (ch % H) * D + ch // H
    partner = (ch % H) * D + (ch // H) // 2 * 2 + (1 - (ch // H) % 2)
    W, bb = np.asarray(L0_attn_W_qkv), np.asarray(L0_attn_b_qkv)
    d = ch // H
    freqs = (10000.0 ** (-2.0 * np.arange(D // 2) / D)).astype(np.float32)
    angles = (np.arange(T, dtype=np.float32)[None, :] * freqs[d // 2][:, None]).astype(np.float32).astype(np.float64)
    sign = np.where(d % 2 == 0, -1.0, 1.0)[:, None]
    tri = np.arange(P)
    bf16 = ml_dtypes.bfloat16
    data = {
        "x": L0_attn_x, "wqs": W[:, 0:C][:, partner], "wks": W[:, C:2 * C][:, partner],
        "wq1": W[:, 0:C][:, by_d], "wk1": W[:, C:2 * C][:, by_d], "wv1": W[:, 2 * C:],
        "bq1": bb[0:C][by_d], "bqs": bb[0:C][partner], "bk1": bb[C:2 * C][by_d], "bks": bb[C:2 * C][partner],
        "bv1": bb[2 * C:], "wp1": L0_attn_W_proj, "bp1": L0_attn_b_proj,
        "ln1g": L0_ffn_ln1_g, "ln1b": L0_ffn_ln1_b, "ln2g": L0_ffn_ln2_g, "ln2b": L0_ffn_ln2_b,
        "wq2": np.asarray(L0_ffn_wq)[:, by_d], "wk2": np.asarray(L0_ffn_wk)[:, by_d], "wv2": L0_ffn_wv,
        "bq2": np.asarray(L0_ffn_bq)[by_d], "bk2": np.asarray(L0_ffn_bk)[by_d], "bv2": L0_ffn_bv,
        "wo2": L0_ffn_wo, "bo2": L0_ffn_bo, "gate_w": L0_ffn_gate_w, "gate_b": L0_ffn_gate_b,
        "w1": L0_ffn_w1, "b1": L0_ffn_b1, "w2": L0_ffn_w2, "b2": L0_ffn_b2,
        "cos": np.cos(angles).astype(np.float32), "sin": (sign * np.sin(angles)).astype(np.float32),
        "key_rows": np.repeat(np.arange(STACK, KROWS) >= MROW, HG * T).reshape(-1, HG * T).astype(bf16),
        "ident": np.eye(P, dtype=np.float32),
        "causal_q": np.where(tri[None, :] > tri[:, None], NEG, 0.0).astype(bf16),
        "causal_k": np.where(tri[:, None] > tri[None, :], NEG, 0.0).astype(bf16),
        "counting": np.tile(np.arange(SLOTS, dtype=np.float32), (P, 1)),
        "zeros": np.zeros((P, C), np.float32),
        "before": np.stack([tri[:, None] < tri[None, :], np.ones((P, P), bool)], 1).astype(np.float32),
    }
    nc = bacc.Bacc("TRN2", target_bir_lowering=False, num_devices=1)
    arrays, aps = {}, {}
    for name, v in data.items():
        v = np.ascontiguousarray(v)
        arrays[f"in_{name}"] = v
        aps[name] = nc.dram_tensor(f"in_{name}", v.shape, mybir.dt.from_np(v.dtype), kind="ExternalInput").ap()
    out = nc.dram_tensor("out_dram", (B, T, C), F32, kind="ExternalOutput").ap()
    build_kernel(nc, out=out, **aps)
    r = run_bass_kernel_spmd(nc, [arrays], core_ids=[0])
    return r.results[0]["out_dram"]
```

```python
from contextlib import ExitStack

import numpy as np

import concourse.bass as bass
from concourse import mybir

F32 = mybir.dt.float32
BF16 = mybir.dt.bfloat16
U32 = mybir.dt.uint32
I32 = mybir.dt.int32
ALU = mybir.AluOpType
ACT = mybir.ActivationFunctionType
AX = mybir.AxisListType

P = 128
B, T, C = 4, 1024, 128
H, D = 16, 8
E, F = 8, 512
NT = T // P
G = 4
HG = H // G
HALF = 512
NPART = 3
STACK = NPART * NPART * D
MROW = 96
KROWS = MROW + NPART
Q_OUT = 16 * NPART * 2
SLOTS = 40
PER = 10
ROUNDS = SLOTS // PER
DIGITS = 5
DEEP = 5
ROW = 3 * C + 1
CLEARS = 8
STACK_IN = 16 * (1 + NPART)
WEIGHTS = ("q1", "qs1", "k1", "ks1", "v1", "o1", "q2", "k2", "v2", "o2")
CONST_PARTS = [("ident", P)] + [(n, C) for n in WEIGHTS] + [("col", 10), ("gate_w", E), ("counting", SLOTS), ("digits", SLOTS)]
CONSTS = sum(width for _, width in CONST_PARTS)
SCALE = float(D) ** -0.5
EPS = 1e-5
NEG = -3.0e38


def attend_steps(causal):
    out = []
    for half in range(T // HALF):
        for kt in range(NT):
            if causal and kt * P >= (half + 1) * HALF:
                continue
            off = max(0, kt * P - half * HALF) if causal else 0
            out.append((half, kt, off, causal and kt * P >= half * HALF))
    return out


def max_units(causal):
    return [(j, qt, P * (qt + 1) if causal else T) for half in range(2) for j in range(HG)
            for qt in range(half * NT // 2, (half + 1) * NT // 2)]


CUTS = ("sum", "0", "1", "2", "3")
SLOTTED = ("max", "turn", "side")


PROLOGUE = ([("stats", "n1"), ("norm", "n1"), ("side", "xt"), ("side", "q"), ("side", "qs"), ("side", "k"), ("side", "ks")]
            + [(kind, *rest) for n in range(len(CUTS)) for kind, rest in (("cut", ("q", CUTS[n])), ("cut", ("k", CUTS[n])))]
            + [("side", "v"), ("out", "q"), ("out", "k"), ("out", "xn")])


VECTOR_COST = {"rec": 900, "stats": 2000, "norm": 2000, ("side", "proj"): 1100, ("side", "v"): 1100,
               ("side", "q"): 1200, ("side", "qs"): 1200, ("side", "k"): 1200, ("side", "ks"): 1200, ("side", "lg"): 2000}


def plan(a, prep, post, clear=False):
    before_q = ["stats n1", "norm n1"] + (["stats n2", "norm n2"] if prep == 2 else [])
    side = {}
    if post:
        early = 4 if a == 1 else 3
        side[0, early] = [("rec",), ("out", "rec")]
        side[0, early + 2] = [("at",)]
        side[0, 7] = [("side", "proj")] + ([("stats", "post")] if post == 1 else [])
        side[0, 8] = ([("norm", "post")] if post == 1 else []) + [("add",)]
        side[0, 9] = [("out", "res")]
        if post == 2:
            side[0, 9] += [("stats", "moe")]
            side[0, 11] = [("norm", "moe")]
            side[0, 12] = [("side", "ht"), ("hn",)]
            side[1, 8] = [("side", "lg"), ("out", "hn")]
    if prep:
        for n, what in enumerate(before_q):
            key = divmod((9 if post == 1 or prep == 1 else 12) + (0, 2, 3, 5)[n], len(attend_steps(a == 1)))
            side[key] = side.get(key, []) + [tuple(what.split())]
        cuts = CUTS[prep == 2:]
        late = 3 * (prep == 2)
        side[1, 1 + late] = side.get((1, 1 + late), []) + [("side", "xt")]
        side[1, 2 + late] = side.get((1, 2 + late), []) + [("side", "q")]
        side[1, 3] = [("side", "qs")] if prep == 1 else [("out", "xn")]
        side[2, 2] = [("out", "q")]
        side[2, 4] = [("side", "k")]
        side[2, 5] = [("side", "ks")] if prep == 1 else []
        side[1, 6 + late] = [("side", "v")]
        for n, what in enumerate(cuts):
            for name, key in (("q", (1, 4 + n + n // 2 + late)), ("k", (2, 6 + n))):
                side[key] = side.get(key, []) + [("cut", name, what)]
        side[2, 11] = side.get((2, 11), []) + [("out", "k"), ("load", 0)]
        side[3, 3] = [("vg", 0), ("vg", 1), ("vg", 2), ("load", 1)]
        side[3, 5] = [("load", 2)]
    if a is None:
        items = [it for key in sorted(side) for it in side[key]]
        if prep:
            items = PROLOGUE + [("load", 0)] + [it for it in items if it[0] == "vg"] + [("load", 1), ("load", 2)]
        if prep:
            items += max_items(0, prep == 1)
        return [(None, [it]) for it in items]
    causal = a == 1
    side[0, 0] = [("vg", G - 1)] + side.get((0, 0), [])
    side[0, 2] = side.get((0, 2), []) + [("load", G - 1)]
    for g in range(G):
        side[g, 1] = [("turn", 1, g)] + side.get((g, 1), [])
        if g:
            side[g, 3] = side.get((g, 3), []) + [("heads", g - 1)]
    for n in range(CLEARS * clear):
        key = (1 + n // 4 * 2, 7 + n % 4 * 2)
        side[key] = side.get(key, []) + [("clear", n)]
    steps = attend_steps(causal)
    pace = np.cumsum([HALF - off + 150 for _, _, off, _ in steps])
    ticks = []
    for g in range(G):
        todo = [side.get((g, s), []) for s in range(len(steps))]
        if prep or g < G - 1:
            causal_next = causal if g < G - 1 else prep == 1
            units = max_items((g + 1) % G, causal_next)
            cost = np.cumsum([0.0] + [keys + 100 for _, _, keys in max_units(causal_next)])
            busy = np.array([sum(VECTOR_COST.get(x, VECTOR_COST.get(x[0], 0)) for x in items) for items in todo])
            room = np.diff(pace, prepend=0) / pace[-1] * (cost[-1] + busy.sum() * 0.75) - busy * 0.75
            pace_g = np.cumsum(np.maximum(room, 1))
            s = 0
            for it in units:
                if it[0] == "max":
                    s = int(np.searchsorted(pace_g / pace_g[-1], (cost[it[2]] + cost[it[2] + 1]) / 2 / cost[-1]))
                todo[s] = todo[s] + [it]
            for s, items in enumerate(todo):
                todo[s] = [it for it in items if it[0] != "norm"] + [it for it in items if it[0] == "norm"]
        for s, (half, kt, off, diag) in enumerate(steps):
            last_kt = max(k for h, k, _, _ in steps if h == half)
            ticks.append(((g, half, kt, off, diag, last_kt, 2 * g + half), todo[s]))
    return ticks


def max_items(g, causal):
    items = []
    for u in range(HG * NT):
        items.append(("max", g, u, causal))
        if u % 16 == 15:
            items.append(("split", u // 16, g, items[-1]))
        if u == 19:
            items.append(("turn", 0, g))
    return items


def build_kernel(nc, x, consts, tables, biases, masks, w1, b1, w2, b2, key_rows, no_token, before, token_ids, out):
    x_t = x.rearrange("b (t p) c -> b p t c", p=P)
    out_rows = out.rearrange("b t c -> (b t) c")

    def scratch(name, shape, dt):
        return nc.dram_tensor(name, shape, dt, kind="Internal").ap()

    q_d = scratch("q_scratch", [NPART, D, G, 2 * HG * HALF], BF16)
    k_d = scratch("k_scratch", [NPART, P, T], BF16)
    heads_d = scratch("heads_scratch", [G, P, T], F32)
    hn_d = scratch("hn_scratch", [B, P, NT, C], F32)
    sorted_d = scratch("sorted_scratch", [SLOTS * P, ROW], F32)
    rec_d = scratch("rec_scratch", [H, T], F32)
    x1_d = scratch("x1_scratch", [B, P, NT, C], F32)
    xn_d = scratch("xn_scratch", [B, P, NT, C], F32)
    xa_d = scratch("xa_scratch", [B, P, NT, C], F32)

    with ExitStack() as whole:
        def sem(name, ctx=whole):
            return ctx.enter_context(nc.semaphore(name))

        def sb(name, shape, dt=F32, ctx=whole):
            return ctx.enter_context(nc.sbuf_tensor(name, shape, dt))

        CONST = sb("CONST", [P, CONSTS])
        place_of, at = {}, 0
        for name, width in CONST_PARTS:
            place_of[name] = CONST[:, at:at + width]
            at += width
        idf, GW, iota, digit_weight = (place_of[n] for n in ("ident", "gate_w", "counting", "digits"))
        wgt = {n: place_of[n] for n in WEIGHTS}
        col = place_of["col"]
        BIAS = sb("BIAS", [P, 6 * C + E])
        rows = BIAS[:, 0:6 * C].rearrange("p (n c) -> p n c", c=C)
        GB = BIAS[:, 6 * C:]
        XT = sb("XT", [P, T])
        XIN = sb("XIN", [P, NT, C])
        XH = sb("XH", [P, NT, C])
        XH2 = sb("XH2", [P, NT, C])
        Y = sb("Y", [P, NT, C])
        RES = sb("RES", [P, NT, C])
        st6 = sb("st6", [P, max(NT, PER), 6])
        mv = sb("mv", [P, max(NT, PER), 2])
        rstd = sb("rstd", [P, max(NT, PER)])
        halfneg = sb("halfneg", [P, NT])
        epsilon = sb("epsilon", [P, 1])
        LG = sb("LG", [P, NT, E])
        top = sb("top", [P, NT, 8])
        pos8 = sb("pos8", [P, NT, 8], U32)
        pos8f = sb("pos8f", [P, NT, 8])
        OHB = sb("OHB", [P, NT, E])
        OH = sb("OH", [P, B, NT * E])
        BQ1, BQS, BK1, BKS, BQ2, BK2, G1, B1, G2, B2 = range(10)

        s_load = sem("s_load")
        s_late = sem("s_late")
        s_init = sem("s_init")
        s_tokens = [sem(f"s_tokens{b}") for b in range(B)]
        s_before, s_sorted, w_in, counted, placed = (
            sem(n) for n in ("s_before", "s_sorted", "w_in", "counted", "placed"))
        s_cleared = sem("s_cleared")

        iteration_sems = []

        def isem(name):
            iteration_sems.append(sem(name))
            return iteration_sems[-1]

        slot_full = [isem(f"slot_full{n}") for n in range(2)]
        slot_free = [isem(f"slot_free{n}") for n in range(2)]
        st_full = isem("st_full")
        exp_done = isem("exp_done")
        av_done = isem("av_done")
        o_evacuated = isem("o_evacuated")
        max_split = isem("max_split")
        rows_in = [isem(f"rows_in{n}") for n in range(2)]
        xin_in, res_in, xn_out, res_out = isem("xin_in"), isem("res_in"), isem("xn_out"), isem("res_out")
        stats_done, rstd_done, norm_done = isem("stats_done"), isem("rstd_done"), isem("norm_done")
        split_done, parts_out = isem("split_done"), isem("parts_out")
        vg_done = isem("vg_done")
        stack_in = [isem(f"stack_in{g}") for g in range(G)]
        heads_in = [isem(f"heads_in{n}") for n in range(2)]
        hn_done, hn_out = isem("hn_done"), isem("hn_out")
        den_in, num_in = isem("den_in"), isem("num_in")
        rec_out, rec_in = isem("rec_out"), isem("rec_in")
        rec_done, at_done, res_done = isem("rec_done"), isem("at_done"), isem("res_done")
        q_cut = isem("q_cut")
        pool_chain, dve_chain = isem("pool_chain"), isem("dve_chain")
        h_full, h_done, y_full, y_used, x_turned, xts_done, fetched = (
            sem(n) for n in ("h_full", "h_done", "y_full", "y_used", "x_turned", "xts_done", "fetched"))
        xa_biased, grouped, measured, eps_added, inverted, y_normed, finished = (
            sem(n) for n in ("xa_biased", "grouped", "measured", "eps_added", "inverted", "y_normed", "finished"))
        xs_in = [sem(f"xs_in{n}") for n in range(PER)]
        rows_out = [sem(f"rows_out{n}") for n in range(PER)]

        def end_iteration():
            nc.all_engine_barrier(sems_to_clear=range(iteration_sems[0].num, iteration_sems[-1].num + 1))

        att = ExitStack()
        QALL = sb("QALL", [KROWS, G, 2, HG, HALF], BF16, att)
        KALL = sb("KALL", [KROWS, G, HG, T], BF16, att)
        QS, KS = [QALL[:, g] for g in range(G)], [KALL[:, g] for g in range(G)]
        VG = [sb(f"VG{g}", [P, NT, HG, 32], F32, att) for g in range(G)]
        PT = sb("PT", [P, 2, HG, HALF], F32, att)
        OT = sb("OT", [P, 2, T], F32, att)
        NUM = sb("NUM", [P, T], F32, att)
        DEN = sb("DEN", [P, P], F32, att)
        REC = sb("REC", [P, T], F32, att)
        T1 = sb("T1", [P, T], F32, att)
        T2 = sb("T2", [P, T], F32, att)
        parts = sb("parts", [P, NPART, T], BF16, att)
        ROT = sb("ROT", [P, 2, T], F32, att)
        VST = sb("VST", [P, NT, C], F32, att)
        idb = sb("idb", [P, P], BF16, att)
        MASKS = sb("MASKS", [P, 2, P], BF16, att)
        mask_q, mask_k = MASKS[:, 0], MASKS[:, 1]
        NM = sb("NM", [P, 2, 16], F32, att)
        NMR = sb("NMR", [P, 2, 16], F32, att)
        NMP = sb("NMP", [P, 2, NPART, 16], BF16, att)
        NMT = sb("NMT", [NPART * 16, 2, P], BF16, att)
        slots = [att.enter_context(nc.psum_tensor(f"slot{n}", [P, T], F32)) for n in range(2)]
        stb = att.enter_context(nc.psum_tensor("stb", [P, 3, HALF], F32))
        OB = att.enter_context(nc.psum_tensor("OB", [P, HALF], F32))
        AT = sb("AT", [P, T], F32, att)
        late_loads = [(MASKS[:], masks), (KALL[STACK:KROWS].rearrange("p g h t -> p (g h t)"), key_rows),
                      (QALL[STACK:MROW].rearrange("p g s h t -> p (g s h t)"), key_rows[0:MROW - STACK])]
        loads = [(CONST[:], consts), (ROT[:], tables), (BIAS[:], biases.unsqueeze(0).to_broadcast([P, 6 * C + E]))]

        with nc.Block() as block:
            @block.sync
            def _(sp):
                for dst, src in loads:
                    sp.dma_start(dst, src).then_inc(s_load, 16)
                sp.dma_start(XIN[:], x_t[0]).then_inc(xin_in, 16)
                for dst, src in late_loads:
                    sp.dma_start(dst, src).then_inc(s_late, 16)
                sp.wait_ge(s_load, 16 * len(loads))

            @block.vector
            def _(dve):
                nc.vector.memset(halfneg[:], -0.5).then_inc(s_init, 1)
                nc.vector.memset(epsilon[:], EPS).then_inc(s_init, 1)
                dve.wait_ge(s_load, 16 * len(loads))
                nc.vector.tensor_copy(idb[:], idf).then_inc(s_init, 1)

            @block.gpsimd
            def _(pool):
                for g in range(G):
                    nc.gpsimd.memset(VG[g][:, :, :, D:D + 1], 1.0)
                    nc.gpsimd.memset(VG[g][:, :, :, D + 1:32], 0.0).then_inc(s_init, 1)
        nc.all_engine_barrier()

        def iteration(a=None, prep=None, prep_b=None, post=None, post_b=None, clear=False):
            ticks = plan(a, prep, post, clear)
            order = [it for _, items in ticks for it in items if it[0] in SLOTTED]
            slot_use = {it: n for n, it in enumerate(order)}
            splits = [it for _, items in ticks for it in items if it[0] == "split"]
            turns = [it for it in order if it[0] == "turn"]
            n_steps = sum(step is not None for step, _ in ticks)
            per_group = n_steps // G

            def slot_of(it):
                return slot_use[it]

            def wait_slot_free(eng, it):
                n = slot_of(it)
                if n >= 2:
                    eng.wait_ge(slot_free[n % 2], n // 2)

            def wait_slot_full(eng, it):
                n = slot_of(it)
                eng.wait_ge(slot_full[n % 2], n // 2 + 1)

            def wait_slot_emptied(eng, it):
                n = slot_of(it)
                eng.wait_ge(slot_free[n % 2], n // 2 + 1)

            def emptied(ins, it):
                ins.then_inc(slot_free[slot_of(it) % 2], 1)

            def slot(it):
                return slots[slot_of(it) % 2]

            norms = [it[1] for _, items in ticks for it in items if it[0] == "stats"]
            norm_src = {"post": Y, "moe": RES, "n1": XIN, "n2": XH}
            norm_dst = {"post": Y, "moe": Y, "n1": XH, "n2": XH2}

            spread = a is None and prep
            cut_bufs = {"q": (T1, T2, parts),
                        "k": (NUM, REC, OT[:].rearrange("p a t -> p (a t)").bitcast(BF16)
                              .rearrange("p (a t) -> p a t", t=T)) if spread else (T1, T2, parts)}
            on_vector = ("sum", "1", "3")

            def cut(eng, it, copy):
                _, name, piece = it
                t1, t2, out3 = cut_bufs[name]
                if piece == "sum":
                    return eng.tensor_tensor(t1[:], t1[:], t2[:], ALU.add)
                if piece == "0":
                    return copy(out3[:, 0, :], t1[:])
                if piece == "1":
                    return eng.tensor_tensor(t1[:], t1[:], out3[:, 0, :], ALU.subtract)
                if piece == "2":
                    return copy(out3[:, 1, :], t1[:])
                return eng.tensor_tensor(out3[:, 2, :], t1[:], out3[:, 1, :], ALU.subtract)

            def units(it):
                return max_units(it[3])[it[2]]

            with nc.Block() as block:
                @block.sync
                def _(sp):
                    ends = {}

                    def load_stack(g):
                        kv = k_d.rearrange("j (d h) t -> (j d) h t", d=D)[:, HG * g:HG * (g + 1), :]
                        kv = kv.rearrange("r h t -> r (h t)").unsqueeze(0).to_broadcast([NPART, NPART * D, HG * T])
                        sp.dma_start(KS[g][0:STACK].rearrange("r h t -> r (h t)"), kv).then_inc(stack_in[g], 16)
                        for i in range(NPART):
                            qv = q_d[i, :, g].unsqueeze(0).to_broadcast([NPART, D, HG * T])
                            sp.dma_start(QS[g][i * NPART * D:(i + 1) * NPART * D].rearrange("r s h t -> r (s h t)"), qv)\
                                .then_inc(stack_in[g], 16)
                        ends[stack_in[g]] = STACK_IN

                    def heads_out(g):
                        if g < G - 1:
                            sp.wait_ge(o_evacuated, 2 * (g + 1))
                        if g == 0 and post:
                            sp.wait_ge(den_in, 16)
                            sp.wait_ge(num_in, 16)
                        sp.dma_start(heads_d[g], OT[:, g % 2, :]).then_inc(heads_in[g % 2], 16)
                        ends[heads_in[g % 2]] = ends.get(heads_in[g % 2], 0) + 16

                    if prep and a:
                        sp.dma_start(XIN[:], x_t[prep_b] if prep == 1 else x1_d[prep_b]).then_inc(xin_in, 16)
                    if post:
                        heads_out(G - 1)
                        sp.wait_ge(heads_in[1], 16)
                        hv = heads_d.rearrange("g (j r) t -> (g j) r t", j=HG)
                        sp.dma_start(DEN[:], hv[:, D, :].rearrange("h (t q) -> h t q", q=P)).then_inc(den_in, 16)
                        sp.dma_start(NUM[:], hv[:, 0:D, :]).then_inc(num_in, 16)
                    for _, items in ticks:
                        for it in items:
                            if it[0] == "turn":
                                _, half, g = it
                                wait_slot_emptied(sp, it)
                                sp.dma_start(QS[g][MROW:KROWS, half].rearrange("p h (t q) -> p (h t) q", q=P),
                                             NMT[:, half, :]).then_inc(rows_in[half], 16)
                                ends[rows_in[half]] = ends.get(rows_in[half], 0) + 16
                            elif it[0] == "load":
                                g = it[1]
                                if g < G - 1:
                                    sp.wait_ge(parts_out, Q_OUT + 16)
                                    if a:
                                        sp.wait_ge(av_done, per_group * (g + 1))
                                load_stack(g)
                            elif it[0] == "heads":
                                heads_out(it[1])
                            elif it[0] == "clear":
                                v = sorted_d.rearrange("(n s p) c -> n s (p c)", n=CLEARS, p=P)[it[1]]
                                sp.dma_start(v, no_token.rearrange("p c -> (p c)").unsqueeze(0)
                                             .to_broadcast([SLOTS // CLEARS, P * ROW])).then_inc(s_cleared, 16)
                            elif it == ("rec",):
                                sp.dma_start(RES[:], x_t[post_b] if post == 1 else xn_d[post_b]).then_inc(res_in, 16)
                            elif it == ("out", "rec"):
                                sp.wait_ge(rec_done, 1)
                                sp.dma_start(rec_d.rearrange("h (t q) -> (h t) q", q=P), DEN[:]).then_inc(rec_out, 16)
                                sp.wait_ge(rec_out, 16)
                                sp.dma_start(REC[:], rec_d.unsqueeze(1).to_broadcast([H, D, T])).then_inc(rec_in, 16)
                                ends[rec_in] = 16
                            elif it[0] == "out":
                                if it[1] == "res":
                                    sp.wait_ge(res_done, 1)
                                    sp.dma_start(x1_d[post_b] if post == 1 else xa_d[post_b], RES[:])\
                                        .then_inc(res_out, 16)
                                    ends[res_out] = 16
                                elif it[1] == "hn":
                                    sp.wait_ge(hn_done, 1)
                                    sp.dma_start(hn_d[post_b], Y[:]).then_inc(hn_out, 16)
                                    ends[hn_out] = 16
                                elif it[1] == "xn":
                                    sp.wait_ge(norm_done, norms.index("n1") + 1)
                                    sp.dma_start(xn_d[prep_b], XH[:]).then_inc(xn_out, 16)
                                    ends[xn_out] = 16
                                else:
                                    n = "qk".index(it[1])
                                    if it[1] == "q" and a:
                                        sp.wait_ge(stack_in[G - 1], STACK_IN)
                                    if spread:
                                        sp.wait_ge(q_cut if n == 0 else split_done, 5 if n == 0 else 1)
                                    else:
                                        sp.wait_ge(split_done, n + 1)
                                    if n:
                                        sp.dma_start(k_d.rearrange("j p t -> p j t"), cut_bufs["k"][2][:, 0:NPART])\
                                            .then_inc(parts_out, 16)
                                    else:
                                        for i in range(NPART):
                                            for half in range(2):
                                                dst = q_d[i].rearrange("d g (s h t) -> (d g) s h t", s=2, t=HALF)
                                                sp.dma_start(dst[:, half],
                                                             parts[:, i, half * HALF:(half + 1) * HALF])\
                                                    .then_inc(parts_out, 16)
                                    ends[parts_out] = Q_OUT + 16 * n
                    for s, n in ends.items():
                        sp.wait_ge(s, n)

                @block.tensor
                def _(pe):
                    def do_max(it):
                        j, qt, keys = units(it)
                        g, causal = it[1], it[3]
                        if a is None:
                            pe.wait_ge(s_late, 16 * len(late_loads))
                        if g in (0, G - 1):
                            pe.wait_ge(stack_in[g], STACK_IN)
                        wait_slot_free(pe, it)
                        w = QS[g][0:MROW, qt // 4, j, qt % 4 * P:(qt % 4 + 1) * P]
                        at = qt * P if causal else T
                        if causal:
                            nc.tensor.matmul(slot(it)[:, at:at + P], w, KS[g][0:MROW, j, at:at + P],
                                             start=True, stop=False)
                            last = nc.tensor.matmul(slot(it)[:, at:at + P], idb[:], mask_q, start=False, stop=True)
                        for c in range(0, min(at, keys), HALF):
                            e = min(c + HALF, at)
                            last = nc.tensor.matmul(slot(it)[:, c:e], w, KS[g][0:MROW, j, c:e], start=True, stop=True)
                        last.then_inc(slot_full[slot_of(it) % 2], 1)

                    def do_turn(it):
                        half = it[1]
                        if (half, it[2]) != (1, 0) or a is None:
                            pe.wait_ge(max_split, [x[1:3] for x in splits].index((half, it[2])) + 1)
                        wait_slot_free(pe, it)
                        nc.tensor.transpose(slot(it)[0:NPART * 16, 0:P // 2].bitcast(BF16),
                                            NMP[:, half, :, :].rearrange("p a b -> p (a b)"), idb[:])\
                            .then_inc(slot_full[slot_of(it) % 2], 1)

                    def do_side(it):
                        name = it[1]
                        wait_slot_free(pe, it)
                        o = slot(it)
                        if name == "xt":
                            pe.wait_ge(norm_done, norms.index("n2" if prep == 2 else "n1") + 1)
                            src = XH2 if prep == 2 else XH
                            for t in range(NT):
                                last = nc.tensor.transpose(o[:, t * P:(t + 1) * P], src[:, t, :], idf)
                        elif name in ("q", "qs", "k", "ks"):
                            wait_slot_emptied(pe, ("side", "xt"))
                            for c in range(0, T, HALF):
                                last = nc.tensor.matmul(o[:, c:c + HALF], wgt[f"{name}{prep}"], XT[:, c:c + HALF],
                                                        start=True, stop=True)
                        elif name == "v":
                            wait_slot_emptied(pe, ("side", "xt"))
                            for t in range(NT):
                                last = nc.tensor.matmul(o[:, t * P:(t + 1) * P], XT[:, t * P:(t + 1) * P],
                                                        wgt[f"v{prep}"], start=True, stop=True)
                        elif name == "ht":
                            pe.wait_ge(norm_done, norms.index("moe") + 1)
                            for t in range(NT):
                                last = nc.tensor.transpose(o[:, t * P:(t + 1) * P], Y[:, t, :], idf)
                        elif name == "lg":
                            wait_slot_emptied(pe, ("side", "ht"))
                            for t in range(NT):
                                last = nc.tensor.matmul(o[:, t * E:(t + 1) * E], T2[:, t * P:(t + 1) * P], GW,
                                                        start=True, stop=True)
                        elif name == "proj":
                            pe.wait_ge(at_done, 1)
                            for t in range(NT):
                                last = nc.tensor.matmul(o[:, t * P:(t + 1) * P], AT[:, t * P:(t + 1) * P],
                                                        wgt[f"o{post}"], start=True, stop=True)
                        last.then_inc(slot_full[slot_of(it) % 2], 1)

                    def item(it):
                        {"max": do_max, "turn": do_turn, "side": do_side}[it[0]](it)

                    def weigh(step, n):
                        g, half, kt, off, _, last_kt, chunk = step
                        pe.wait_ge(exp_done, HG * (n + 1))
                        if kt == 0 and chunk >= 1:
                            pe.wait_ge(o_evacuated, chunk)
                        if chunk == 2 * (G - 1) and kt == 0:
                            pe.wait_ge(vg_done, 1)
                        for j in range(HG):
                            last = nc.tensor.matmul(OB[32 * j:32 * j + 32, off:HALF], VG[g][:, kt, j, :],
                                                    PT[:, n % 2, j, off:HALF], start=(kt == 0), stop=(kt == last_kt),
                                                    skip_group_check=True)
                        last.then_inc(av_done, 1)

                    before = None
                    n = 0
                    for step, items in ticks:
                        mine = [it for it in items if it[0] in SLOTTED]
                        if step is None:
                            for it in mine:
                                item(it)
                            continue
                        g, half, kt, off, diag, last_kt, chunk = step
                        if kt == 0:
                            if g + half:
                                pe.wait_ge(rows_in[half], 16 * (g + half))
                        for j in range(HG):
                            m = HG * n + j
                            if m >= 3:
                                pe.wait_ge(exp_done, m - 2)
                            o = stb[:, m % 3, :]
                            w = KS[g][:, j, kt * P:(kt + 1) * P]
                            if diag:
                                nc.tensor.matmul(o[:, off:off + P], w, QS[g][:, half, j, off:off + P], start=True, stop=False)
                                last = nc.tensor.matmul(o[:, off:off + P], idb[:], mask_k, start=False, stop=True)
                                if off + P < HALF:
                                    last = nc.tensor.matmul(o[:, off + P:HALF], w,
                                                            QS[g][:, half, j, off + P:HALF], start=True, stop=True)
                            else:
                                last = nc.tensor.matmul(o[:, off:HALF], w, QS[g][:, half, j, off:HALF],
                                                        start=True, stop=True)
                            last.then_inc(st_full, 1)
                            if j == 0 and mine:
                                item(mine[0])
                            if j == 2:
                                if mine[1:]:
                                    item(mine[1])
                                if before is not None:
                                    weigh(before, n - 1)
                                if mine[2:]:
                                    item(mine[2])
                        for it in mine[3:]:
                            item(it)
                        before = step
                        n += 1
                    if before is not None:
                        weigh(before, n - 1)

                @block.scalar
                def _(act):
                    def evacuate(chunk):
                        g, half = divmod(chunk, 2)
                        gone = sum(h % 2 == g % 2 for h in ([G - 1] if post else []) + list(range(g)))
                        if half == 0 and gone:
                            act.wait_ge(heads_in[g % 2], 16 * gone)
                        nc.scalar.copy(OT[:, g % 2, half * HALF:(half + 1) * HALF], OB[:]).then_inc(o_evacuated, 1)

                    def empty_slots(items):
                        for it in items:
                            if it[0] == "cut" and spread and it[1] == "q" and it[2] not in on_vector:
                                act.wait_ge(q_cut, CUTS.index(it[2]))
                                cut(nc.scalar, it, nc.scalar.copy).then_inc(q_cut, 1)
                            elif it[0] == "turn":
                                wait_slot_full(act, it)
                                before = sum(x[1] == it[1] for x in turns[:turns.index(it)])
                                if before:
                                    act.wait_ge(rows_in[it[1]], 16 * before)
                                emptied(nc.scalar.copy(NMT[:, it[1], :],
                                                       slot(it)[0:NPART * 16, 0:P // 2].bitcast(BF16)), it)
                            elif prep == 2 and it in (("side", "q"), ("side", "k")):
                                wait_slot_full(act, it)
                                if it[1] == "k":
                                    act.wait_ge(split_done, 1)
                                c = BQ2 if it[1] == "q" else BK2
                                emptied(nc.scalar.activation(T1[:], slot(it)[:], ACT.Identity,
                                                             bias=col[:, c:c + 1]), it)
                            elif it == ("side", "ht"):
                                wait_slot_full(act, it)
                                emptied(nc.scalar.activation(T2[:], slot(it)[:], ACT.Identity,
                                                             bias=col[:, B2:B2 + 1], scale=col[:, G2:G2 + 1]), it)
                            elif it == ("side", "xt"):
                                wait_slot_full(act, it)
                                if prep == 1:
                                    emptied(nc.scalar.copy(XT[:], slot(it)[:]), it)
                                else:
                                    emptied(nc.scalar.activation(XT[:], slot(it)[:], ACT.Identity,
                                                                 bias=col[:, B1:B1 + 1], scale=col[:, G1:G1 + 1]), it)

                    n = 0
                    done = None
                    for step, items in ticks:
                        if step is not None:
                            g, half, kt, off, diag, last_kt, chunk = step
                            for j in range(HG):
                                m = HG * n + j
                                act.wait_ge(st_full, m + 1)
                                if j == 0 and n >= 2:
                                    act.wait_ge(av_done, n - 1)
                                nc.scalar.activation(PT[:, n % 2, j, off:HALF], stb[:, m % 3, off:HALF], ACT.Exp,
                                                     scale=SCALE).then_inc(exp_done, 1)
                                if j == 1:
                                    empty_slots(items)
                            if done is not None:
                                act.wait_ge(av_done, n)
                                evacuate(done)
                                done = None
                            if kt == last_kt:
                                done = chunk
                            n += 1
                        if step is None:
                            empty_slots(items)
                    if done is not None:
                        act.wait_ge(av_done, n)
                        evacuate(done)

                @block.vector
                def _(dve):
                    links = [0]

                    def link(ins):
                        links[0] += 1
                        ins.then_inc(dve_chain, 1)
                        dve.wait_ge(dve_chain, links[0])

                    for it in (it for _, items in ticks for it in items):
                        if it[0] == "max":
                            j, qt, keys = units(it)
                            half = it[2] // 16
                            if it[2] % 16 == 0:
                                before = [n for n, x in enumerate(splits) if x[1] == half
                                          and splits.index(next(y for y in splits if y[1:3] == (half, it[1]))) > n]
                                if before:
                                    dve.wait_ge(max_split, before[-1] + 1)
                            wait_slot_full(dve, it)
                            at = j * 4 + qt % 4
                            emptied(nc.vector.tensor_reduce(NM[:, half, at:at + 1], slot(it)[:, 0:keys], AX.X,
                                                            ALU.max, negate=True), it)
                        elif it[0] == "rec":
                            dve.wait_ge(den_in, 16)
                            nc.vector.reciprocal(DEN[:], DEN[:]).then_inc(rec_done, 1)
                        elif it == ("side", "proj"):
                            wait_slot_full(dve, it)
                            bias = rows[:, 1 if post == 1 else 3, :].unsqueeze(1).to_broadcast([P, NT, C])
                            emptied(nc.vector.tensor_tensor(Y[:], slot(it)[:].rearrange("p (t c) -> p t c", t=NT),
                                                            bias, ALU.add), it)
                        elif it[0] == "at" and a is None:
                            dve.wait_ge(num_in, 16)
                            dve.wait_ge(rec_in, 16)
                            nc.vector.tensor_tensor(AT[:], NUM[:], REC[:], ALU.mult).then_inc(at_done, 1)
                        elif it[0] == "add" and a is None:
                            dve.wait_ge(res_in, 16)
                            wait_slot_emptied(dve, ("side", "proj"))
                            nc.vector.tensor_tensor(RES[:], RES[:], Y[:], ALU.add).then_inc(res_done, 1)
                        elif it[0] == "stats":
                            src = norm_src[it[1]]
                            if it[1] == "post":
                                wait_slot_emptied(dve, ("side", "proj"))
                            elif it[1] == "moe":
                                dve.wait_ge(res_done, 1)
                            elif it[1] == "n1":
                                dve.wait_ge(xin_in, 16)
                            else:
                                dve.wait_ge(norm_done, norms.index("n1") + 1)
                            for t in range(NT):
                                last = nc.vector.bn_stats(st6[:, t, :], src[:, t, :])
                            link(last)
                            for t in range(NT):
                                last = nc.vector.bn_aggr(mv[:, t, :], st6[:, t, :])
                            last.then_inc(stats_done, 1)
                        elif it[0] == "norm":
                            dve.wait_ge(rstd_done, norms.index(it[1]) + 1)
                            for t in range(NT):
                                last = nc.vector.tensor_scalar(norm_dst[it[1]][:, t, :], norm_src[it[1]][:, t, :],
                                                               mv[:, t, 0:1], rstd[:, t:t + 1],
                                                               ALU.subtract, ALU.mult)
                            last.then_inc(norm_done, 1)
                        elif prep == 1 and it[0] == "side" and it[1] in ("q", "k", "qs", "ks"):
                            wait_slot_full(dve, it)
                            if it[1] == "k" and not spread:
                                dve.wait_ge(split_done, 1)
                            rot_a, rot_b, _ = cut_bufs[it[1][0]]
                            c = {"q": BQ1, "qs": BQS, "k": BK1, "ks": BKS}[it[1]]
                            dst, table = (rot_b, ROT[:, 1]) if it[1][1:] else (rot_a, ROT[:, 0])
                            emptied(nc.vector.scalar_tensor_tensor(dst[:], slot(it)[:], col[:, c:c + 1], table,
                                                                   ALU.add, ALU.mult), it)
                        elif it == ("side", "lg"):
                            wait_slot_full(dve, it)
                            emptied(nc.vector.tensor_tensor(LG[:], slot(it)[:, 0:NT * E]
                                                            .rearrange("p (t e) -> p t e", t=NT),
                                                            GB.unsqueeze(1).to_broadcast([P, NT, E]), ALU.add), it)
                            wait_slot_emptied(dve, it)
                            for t in range(NT):
                                last = nc.vector.max(top[:, t, :], LG[:, t, :])
                            link(last)
                            for t in range(NT):
                                last = nc.vector.max_index(pos8[:, t, :], top[:, t, :], LG[:, t, :])
                            link(last)
                            link(nc.vector.tensor_copy(pos8f[:], pos8[:]))
                            link(nc.vector.tensor_tensor(OHB[:], pos8f[:, :, 0:1].to_broadcast([P, NT, E]),
                                                         iota[:, 0:E].unsqueeze(1).to_broadcast([P, NT, E]),
                                                         ALU.is_equal))
                            link(nc.vector.tensor_copy(OH[:, post_b], OHB[:].rearrange("p t e -> p (t e)")))
                        elif it[0] == "cut" and spread and it[1] == "q" and it[2] in on_vector:
                            piece = CUTS.index(it[2])
                            if piece:
                                dve.wait_ge(q_cut, piece)
                            else:
                                wait_slot_emptied(dve, ("side", "qs"))
                            cut(nc.vector, it, None).then_inc(q_cut, 1)
                        elif it == ("side", "v"):
                            wait_slot_full(dve, it)
                            if a:
                                dve.wait_ge(vg_done, 1)
                            bias = rows[:, 0 if prep == 1 else 2, :].unsqueeze(1).to_broadcast([P, NT, C])
                            emptied(nc.vector.tensor_tensor(VST[:], slot(it)[:].rearrange("p (t c) -> p t c", t=NT),
                                                            bias, ALU.add), it)

                @block.gpsimd
                def _(pool):
                    links = [0]

                    def link(ins):
                        links[0] += 1
                        ins.then_inc(pool_chain, 1)
                        pool.wait_ge(pool_chain, links[0])

                    def rounded(dst, src):
                        return nc.gpsimd.tensor_scalar(dst, src, 1.0, 0.0, ALU.mult, ALU.add)

                    for it in (it for _, items in ticks for it in items):
                        if it[0] == "split":
                            _, half, g, last = it
                            wait_slot_emptied(pool, last)
                            before = [t for t in turns if t[1] == half and order.index(t) < order.index(last)]
                            if before:
                                wait_slot_full(pool, before[-1])
                            link(rounded(NMP[:, half, 0, :], NM[:, half, :]))
                            link(nc.gpsimd.tensor_tensor(NMR[:, half, :], NM[:, half, :], NMP[:, half, 0, :],
                                                         ALU.subtract))
                            link(rounded(NMP[:, half, 1, :], NMR[:, half, :]))
                            nc.gpsimd.tensor_tensor(NMP[:, half, 2, :], NMR[:, half, :], NMP[:, half, 1, :],
                                                    ALU.subtract).then_inc(max_split, 1)
                        elif it[0] == "vg":
                            g = it[1]
                            if g < G - 1:
                                wait_slot_emptied(pool, ("side", "v"))
                                if a:
                                    pool.wait_ge(av_done, per_group * (g + 1))
                            nc.gpsimd.tensor_copy(VG[g][:, :, :, 0:D],
                                                  VST[:, :, g * HG * D:(g + 1) * HG * D]
                                                  .rearrange("p t (j d) -> p t j d", d=D)).then_inc(vg_done, 1)
                        elif it[0] == "at" and a:
                            pool.wait_ge(num_in, 16)
                            pool.wait_ge(rec_in, 16)
                            nc.gpsimd.tensor_tensor(AT[:], NUM[:], REC[:], ALU.mult).then_inc(at_done, 1)
                        elif it[0] == "hn":
                            wait_slot_full(pool, ("side", "ht"))
                            for n, op in ((4, ALU.mult), (5, ALU.add)):
                                ins = nc.gpsimd.tensor_tensor(Y[:], Y[:], rows[:, n, :].unsqueeze(1)
                                                              .to_broadcast([P, NT, C]), op)
                                if n == 4:
                                    link(ins)
                            ins.then_inc(hn_done, 1)
                        elif it[0] == "add" and a:
                            pool.wait_ge(res_in, 16)
                            if post == 1:
                                pool.wait_ge(norm_done, norms.index("post") + 1)
                            else:
                                wait_slot_emptied(pool, ("side", "proj"))
                            nc.gpsimd.tensor_tensor(RES[:], RES[:], Y[:], ALU.add).then_inc(res_done, 1)
                        elif it[0] == "stats":
                            pool.wait_ge(stats_done, norms.index(it[1]) + 1)
                            link(nc.gpsimd.tensor_scalar(rstd[:, 0:NT], mv[:, 0:NT, 1], EPS, None, ALU.add))
                            nc.gpsimd.tensor_tensor(rstd[:, 0:NT], rstd[:, 0:NT], halfneg[:], ALU.pow).then_inc(rstd_done, 1)
                        elif it[0] == "cut" and not (spread and it[1] == "q"):
                            _, name, piece = it
                            if piece == "sum":
                                wait_slot_emptied(pool, ("side", name))
                                wait_slot_emptied(pool, ("side", name + "s"))
                            elif piece == "0":
                                if prep == 2:
                                    wait_slot_emptied(pool, ("side", name))
                                if name == "k" and not spread:
                                    pool.wait_ge(parts_out, Q_OUT)
                            ins = cut(nc.gpsimd, it, rounded)
                            if piece == "3":
                                ins.then_inc(split_done, 1)
                            else:
                                link(ins)
            end_iteration()

        iteration(prep=1, prep_b=0)
        iteration(a=1, prep=1, prep_b=1)
        with nc.Fori(1, B - 1) as b:
            iteration(a=1, prep=1, prep_b=b + 1, post=1, post_b=b - 1)
        iteration(a=1, prep=2, prep_b=0, post=1, post_b=B - 2)
        iteration(a=2, prep=2, prep_b=1, post=1, post_b=B - 1, clear=True)
        with nc.Fori(1, B - 1) as b:
            iteration(a=2, prep=2, prep_b=b + 1, post=2, post_b=b - 1)
        iteration(a=2, post=2, post_b=B - 2)
        iteration(post=2, post_b=B - 1)
        att.close()

        moe = ExitStack()
        NF = F // P
        WIDE = F + F + C + NF
        W = sb("W", [P, E, WIDE], F32, moe)
        WS = sb("WS", [P, DEEP, WIDE], F32, moe)
        BF = sb("BF", [P, 2, P], F32, moe)
        IDS = sb("IDS", [P, B * NT], U32, moe)
        TOK = sb("TOK", [P, B * NT, ROW], F32, moe)
        ones = sb("ones", [P, B * NT], F32, moe)
        cnt = sb("cnt", [P, B * NT, E], F32, moe)
        upto = sb("upto", [P, B * NT, E], F32, moe)
        place = sb("place", [P, B * NT, E], F32, moe)
        need = sb("need", [P, E], F32, moe)
        needi = sb("needi", [P, E], I32, moe)
        tiles = sb("tiles", [P, E], F32, moe)
        tiles_upto = sb("tiles_upto", [P, E], F32, moe)
        first = sb("first", [P, E], F32, moe)
        spot = sb("spot", [P, B * NT], F32, moe)
        spoti = sb("spoti", [P, B * NT], U32, moe)
        passed = sb("passed", [P, SLOTS, E - 1], F32, moe)
        owner = sb("owner", [P, SLOTS], F32, moe)
        packedf = sb("packedf", [P, SLOTS // DIGITS], F32, moe)
        packed = sb("packed", [P, SLOTS // DIGITS], I32, moe)
        pR = moe.enter_context(nc.psum_tensor("pR", [P, 2, HALF], F32))

        w_loads = [(W[:, :, 0:F], w1.rearrange("e c f -> c e f"))]
        w_loads += [(W[:, e, F:2 * F].rearrange("p (f c) -> p f c", f=NF), w2[e].rearrange("(p f) c -> p f c", f=NF))
                    for e in range(E)]
        w_loads += [(W[:, :, 2 * F:2 * F + C], b2.unsqueeze(0).to_broadcast([P, E, C]))]
        w_loads += [(W[:, e, 2 * F + C:WIDE], b1[e].rearrange("(p f) -> p f", f=NF)) for e in range(E)]

        with nc.Block() as block:
            @block.sync
            def _(sp):
                sp.dma_start(BF[:], before).then_inc(s_before, 16)
                sp.dma_start(IDS[:], token_ids).then_inc(s_before, 16)
                for b in range(B):
                    for n, src in enumerate((hn_d, xa_d, x1_d)):
                        sp.dma_start(TOK[:, b * NT:(b + 1) * NT, n * C:(n + 1) * C], src[b])\
                            .then_inc(s_tokens[b], 16)
                for dst, src in w_loads:
                    sp.dma_start(dst, src).then_inc(w_in, 16)
                sp.wait_ge(w_in, 16 * len(w_loads))

            @block.tensor
            def _(pe):
                pe.wait_ge(s_before, 32)
                for n in range(2):
                    nc.tensor.matmul(pR[:, n, 0:B * NT * E], BF[:, n, :], OH[:].rearrange("p b te -> p (b te)"),
                                     start=True, stop=True).then_inc(counted, 1)

            @block.vector
            def _(dve):
                links = [0]

                def link(ins):
                    links[0] += 1
                    ins.then_inc(dve_chain, 1)
                    dve.wait_ge(dve_chain, links[0])

                link(nc.vector.memset(ones[:], 1.0))
                dve.wait_ge(counted, 2)
                link(nc.vector.tensor_copy(cnt[:], pR[:, 1, 0:B * NT * E].rearrange("p (t e) -> p t e", e=E)))
                for e in range(E):
                    last = nc.vector.tensor_tensor_scan(upto[:, :, e], ones[:], cnt[:, :, e], 0.0, ALU.mult, ALU.add)
                link(last)
                link(nc.vector.tensor_scalar(needi[:], upto[:, B * NT - 1, :], float(P - 1), None, ALU.add))
                link(nc.vector.tensor_scalar(needi[:], needi[:], 7, None, ALU.arith_shift_right))
                link(nc.vector.tensor_copy(tiles[:], needi[:]))
                link(nc.vector.tensor_tensor_scan(tiles_upto[:], ones[:, 0:E], tiles[:], 0.0, ALU.mult, ALU.add))
                link(nc.vector.tensor_tensor(first[:], tiles_upto[:], tiles[:], ALU.subtract))
                link(nc.vector.tensor_tensor(place[:], upto[:], cnt[:], ALU.subtract))
                link(nc.vector.tensor_tensor(place[:], pR[:, 0, 0:B * NT * E].rearrange("p (t e) -> p t e", e=E),
                                             place[:], ALU.add))
                link(nc.vector.tensor_scalar(need[:], first[:], float(P), None, ALU.mult))
                link(nc.vector.tensor_tensor(place[:], place[:], need[:].unsqueeze(1).to_broadcast([P, B * NT, E]),
                                             ALU.add))
                link(nc.vector.tensor_tensor(place[:], place[:], OH[:].rearrange("p b (t e) -> p (b t) e", e=E),
                                             ALU.mult))
                link(nc.vector.tensor_reduce(spot[:], place[:], AX.X, ALU.add))
                link(nc.vector.tensor_copy(spoti[:], spot[:]))
                dve.wait_ge(s_before, 32)
                nc.vector.tensor_copy(TOK[:, :, 3 * C:].bitcast(U32), IDS[:].unsqueeze(2)).then_inc(placed, 1)
                link(nc.vector.tensor_tensor(passed[:], iota.unsqueeze(2).to_broadcast([P, SLOTS, E - 1]),
                                             first[:, 1:E].unsqueeze(1).to_broadcast([P, SLOTS, E - 1]), ALU.is_ge))
                link(nc.vector.tensor_reduce(owner[:], passed[:], AX.X, ALU.add))
                link(nc.vector.tensor_tensor(owner[:], owner[:], digit_weight, ALU.mult))
                link(nc.vector.tensor_reduce(packedf[:], owner[:].rearrange("p (w k) -> p w k", k=DIGITS), AX.X,
                                             ALU.add))
                link(nc.vector.tensor_copy(packed[:], packedf[:]))

            @block.gpsimd
            def _(pool):
                pool.wait_ge(placed, 1)
                pool.wait_ge(s_cleared, 16 * CLEARS)
                for t in range(B * NT):
                    if t % NT == 0:
                        pool.wait_ge(s_tokens[t // NT], 16 * 3)
                    nc.gpsimd.indirect_dma_start(
                        out=sorted_d, out_offset=bass.IndirectOffsetOnAxis(ap=spoti[:, t:t + 1], axis=0),
                        in_=TOK[:, t, :], in_offset=None).then_inc(s_sorted, 16)
                pool.wait_ge(s_sorted, 16 * B * NT)
        end_iteration()

        slot_mem = ExitStack()
        XS = sb("XS", [P, PER, ROW], F32, slot_mem)
        XTS = sb("XTS", [P, 2, P], F32, slot_mem)
        MID = sb("MID", [P, 2, F], F32, slot_mem)
        YS = sb("YS", [P, PER, C], F32, slot_mem)
        pX = slot_mem.enter_context(nc.psum_tensor("pX", [P, 2, HALF], F32))
        pH = slot_mem.enter_context(nc.psum_tensor("pH", [P, 2, HALF], F32))
        pY = slot_mem.enter_context(nc.psum_tensor("pY", [P, 2, HALF], F32))
        sorted_v = sorted_d.rearrange("(i s p) c -> i p s c", p=P, s=PER)

        def pipeline(eng, stages, begin=None):
            def round_of(i, first, second):
                if begin:
                    begin(i)
                for u in range(PER):
                    for stage, lag in stages:
                        if u >= lag:
                            stage(i, u - lag, first)
                        elif not first:
                            stage(i - 1, u - lag + PER, second)

            round_of(0, True, False)
            round_of(1, False, True)
            with eng.Fori(2, ROUNDS) as i:
                round_of(i, False, False)
            for u in range(max(lag for _, lag in stages)):
                for stage, lag in stages:
                    if lag > u:
                        stage(ROUNDS - 1, PER + u - lag, False)

        with nc.Block() as block:
            @block.sync
            def _(sp):
                def load(i, u):
                    sp.dma_start(XS[:, u, :], sorted_v[i][:, u, :]).then_inc(xs_in[u], 16)

                for u in range(PER):
                    load(0, u)
                with sp.Fori(1, ROUNDS) as i:
                    for u in range(PER):
                        sp.wait_ge(rows_out[u], i * 16)
                        load(i, u)
                for u in range(PER):
                    sp.wait_ge(rows_out[u], 16 * ROUNDS)

            @block.vector
            def _(dve):
                experts = []

                def look_up(i):
                    for w in range(PER // DIGITS):
                        word = dve.value_load(packed[0:1, bass.ds(i * (PER // DIGITS) + w, 1)],
                                              min_val=0, max_val=E ** DIGITS - 1)
                        for k in range(DIGITS):
                            experts[w * DIGITS + k:] = [word // E ** k % E]

                def add(i, u, first):
                    dve.wait_ge(y_full, i * PER + u + 1)
                    dve.wait_ge(xa_biased, i * PER + u + 1)
                    nc.vector.tensor_tensor(YS[:, u, :], pY[:, u % 2, 0:C], XS[:, u, C:2 * C], ALU.add)\
                        .then_inc(y_used, 1)

                def fetch(i, u, first):
                    nc.vector.tensor_copy(WS[:, u % DEEP, :],
                                          W[:, bass.ds(experts[u], 1), :].rearrange("p o w -> p (o w)"))\
                        .then_inc(fetched, 1)

                def stats(i, u, first):
                    dve.wait_ge(y_used, i * PER + u + 1)
                    nc.vector.bn_stats(st6[:, u, :], YS[:, u, :]).then_inc(grouped, 1)

                def norm(i, u, first):
                    dve.wait_ge(inverted, i * PER + u + 1)
                    nc.vector.tensor_scalar(YS[:, u, :], YS[:, u, :], mv[:, u, 0:1], rstd[:, u:u + 1],
                                            ALU.subtract, ALU.mult).then_inc(y_normed, 1)

                def grouped_in(i, u, first):
                    dve.wait_ge(grouped, i * PER + u + 1)

                def aggregate(i, u, first):
                    nc.vector.bn_aggr(mv[:, u, :], st6[:, u, :]).then_inc(measured, 1)

                def bias(i, u, first):
                    dve.wait_ge(xs_in[u], (i + 1) * 16)
                    dve.wait_ge(fetched, i * PER + u + 1)
                    nc.vector.tensor_tensor(XS[:, u, C:2 * C], XS[:, u, C:2 * C],
                                            WS[:, u % DEEP, 2 * F:2 * F + C], ALU.add).then_inc(xa_biased, 1)

                def finish(i, u, first):
                    dve.wait_ge(y_normed, i * PER + u + 1)
                    nc.vector.tensor_tensor(YS[:, u, :], YS[:, u, :], XS[:, u, 2 * C:3 * C], ALU.add)\
                        .then_inc(finished, 1)

                pipeline(dve, [(add, 3), (bias, 1), (stats, 3), (fetch, 0), (grouped_in, 3), (norm, 4),
                               (aggregate, 3), (finish, 4)], look_up)

            @block.gpsimd
            def _(pool):
                def inverse(i, u, first):
                    pool.wait_ge(measured, i * PER + u + 1)
                    nc.gpsimd.tensor_tensor(rstd[:, u:u + 1], mv[:, u, 1:2], epsilon[:], ALU.add)\
                        .then_inc(eps_added, 1)
                    pool.wait_ge(eps_added, i * PER + u + 1)
                    nc.gpsimd.tensor_tensor(rstd[:, u:u + 1], rstd[:, u:u + 1], halfneg[:, 0:1], ALU.pow)\
                        .then_inc(inverted, 1)

                def finished_in(i, u, first):
                    pool.wait_ge(finished, i * PER + u + 1)

                def send(i, u, first):
                    nc.gpsimd.indirect_dma_start(
                        out=out_rows, out_offset=bass.IndirectOffsetOnAxis(ap=XS[:, u, 3 * C:].bitcast(U32), axis=0),
                        in_=YS[:, u, :], in_offset=None, bounds_check=B * T - 1, oob_is_err=False)\
                        .then_inc(rows_out[u], 16)

                pipeline(pool, [(finished_in, 4), (inverse, 3), (send, 4)])

            @block.scalar
            def _(act):
                def turned(i, u, first):
                    act.wait_ge(x_turned, i * PER + u + 1)
                    if not (first and u < 2):
                        act.wait_ge(h_full, i * PER + u - 1)
                    nc.scalar.copy(XTS[:, u % 2, :], pX[:, u % 2, 0:P]).then_inc(xts_done, 1)

                def relu(i, u, first):
                    act.wait_ge(h_full, i * PER + u + 1)
                    if not (first and u < 2):
                        act.wait_ge(y_full, i * PER + u - 1)
                    for f in range(NF):
                        at = 2 * F + C + f
                        last = nc.scalar.activation(MID[:, u % 2, f * P:(f + 1) * P],
                                                    pH[:, u % 2, f * P:(f + 1) * P], ACT.Relu,
                                                    bias=WS[:, u % DEEP, at:at + 1])
                    last.then_inc(h_done, 1)

                pipeline(act, [(turned, 0), (relu, 1)])

            @block.tensor
            def _(pe):
                def turn(i, u, first):
                    pe.wait_ge(xs_in[u], (i + 1) * 16)
                    if not (first and u < 2):
                        pe.wait_ge(xts_done, i * PER + u - 1)
                    nc.tensor.transpose(pX[:, u % 2, 0:P], XS[:, u, 0:C], idf).then_inc(x_turned, 1)

                def hidden(i, u, first):
                    pe.wait_ge(xts_done, i * PER + u + 1)
                    pe.wait_ge(fetched, i * PER + u + 1)
                    if not (first and u < 2):
                        pe.wait_ge(h_done, i * PER + u - 1)
                    for f in range(NF):
                        w_f = WS[:, u % DEEP, 0:F].rearrange("c (p f) -> c f p", f=NF)[:, f, :]
                        last = nc.tensor.matmul(pH[:, u % 2, f * P:(f + 1) * P], w_f, XTS[:, u % 2, :],
                                                start=True, stop=True)
                    last.then_inc(h_full, 1)

                def back(i, u, first):
                    pe.wait_ge(h_done, i * PER + u + 1)
                    if not (first and u < 2):
                        pe.wait_ge(y_used, i * PER + u - 1)
                    for f in range(NF):
                        last = nc.tensor.matmul(pY[:, u % 2, 0:C], MID[:, u % 2, f * P:(f + 1) * P],
                                                WS[:, u % DEEP, F + f * C:F + (f + 1) * C],
                                                start=(f == 0), stop=(f == NF - 1))
                    last.then_inc(y_full, 1)

                pipeline(pe, [(turn, 0), (hidden, 1), (back, 2)])
        slot_mem.close()
        moe.close()


def kernel(L0_attn_x, L0_attn_W_qkv, L0_attn_b_qkv, L0_attn_W_proj, L0_attn_b_proj, L0_ffn_ln1_g, L0_ffn_ln1_b,
           L0_ffn_ln2_g, L0_ffn_ln2_b, L0_ffn_wq, L0_ffn_bq, L0_ffn_wk, L0_ffn_bk, L0_ffn_wv, L0_ffn_bv, L0_ffn_wo,
           L0_ffn_bo, L0_ffn_gate_w, L0_ffn_gate_b, L0_ffn_w1, L0_ffn_b1, L0_ffn_w2, L0_ffn_b2):
    import concourse.bacc as bacc
    from concourse.bass_utils import run_bass_kernel_spmd
    import ml_dtypes

    ch = np.arange(C)
    by_d = (ch % H) * D + ch // H
    partner = (ch % H) * D + (ch // H) // 2 * 2 + (1 - (ch // H) % 2)
    W, bb = np.asarray(L0_attn_W_qkv), np.asarray(L0_attn_b_qkv)
    d = ch // H
    freqs = (10000.0 ** (-2.0 * np.arange(D // 2) / D)).astype(np.float32)
    angles = (np.arange(T, dtype=np.float32)[None, :] * freqs[d // 2][:, None]).astype(np.float32).astype(np.float64)
    sign = np.where(d % 2 == 0, -1.0, 1.0)[:, None]
    tri = np.arange(P)
    bf16 = ml_dtypes.bfloat16
    consts = {
        "ident": np.eye(P, dtype=np.float32),
        "qs1": W[:, 0:C][:, partner], "ks1": W[:, C:2 * C][:, partner],
        "q1": W[:, 0:C][:, by_d], "k1": W[:, C:2 * C][:, by_d], "v1": W[:, 2 * C:], "o1": L0_attn_W_proj,
        "q2": np.asarray(L0_ffn_wq)[:, by_d], "k2": np.asarray(L0_ffn_wk)[:, by_d], "v2": L0_ffn_wv, "o2": L0_ffn_wo,
        "col": np.stack([bb[0:C][by_d], bb[0:C][partner], bb[C:2 * C][by_d], bb[C:2 * C][partner],
                         np.asarray(L0_ffn_bq)[by_d], np.asarray(L0_ffn_bk)[by_d],
                         L0_ffn_ln1_g, L0_ffn_ln1_b, L0_ffn_ln2_g, L0_ffn_ln2_b], 1),
        "gate_w": L0_ffn_gate_w, "counting": np.tile(np.arange(SLOTS, dtype=np.float32), (P, 1)),
        "digits": np.tile(np.float32(E) ** (np.arange(SLOTS) % DIGITS), (P, 1)).astype(np.float32),
    }
    data = {
        "x": L0_attn_x, "w1": L0_ffn_w1, "b1": L0_ffn_b1, "w2": L0_ffn_w2, "b2": L0_ffn_b2,
        "consts": np.concatenate([consts[n] for n, _ in CONST_PARTS], 1),
        "tables": np.stack([np.cos(angles), sign * np.sin(angles)], 1).astype(np.float32),
        "biases": np.concatenate([bb[2 * C:], L0_attn_b_proj, L0_ffn_bv, L0_ffn_bo, L0_ffn_ln2_g, L0_ffn_ln2_b,
                                  L0_ffn_gate_b]),
        "key_rows": np.repeat(np.arange(STACK, KROWS) >= MROW, G * HG * T).reshape(-1, G * HG * T).astype(bf16),
        "masks": np.stack([np.where(tri[None, :] > tri[:, None], NEG, 0.0),
                           np.where(tri[:, None] > tri[None, :], NEG, 0.0)], 1).astype(bf16),
        "no_token": np.concatenate([np.zeros((P, ROW - 1), np.uint32), np.full((P, 1), B * T, np.uint32)], 1)
        .view(np.float32),
        "token_ids": (np.arange(B * T // P)[None, :] * P + tri[:, None]).astype(np.uint32),
        "before": np.stack([tri[:, None] < tri[None, :], np.ones((P, P), bool)], 1).astype(np.float32),
    }
    nc = bacc.Bacc("TRN2", target_bir_lowering=False, num_devices=1)
    arrays, aps = {}, {}
    for name, v in data.items():
        v = np.ascontiguousarray(v)
        arrays[f"in_{name}"] = v
        aps[name] = nc.dram_tensor(f"in_{name}", v.shape, mybir.dt.from_np(v.dtype), kind="ExternalInput").ap()
    out = nc.dram_tensor("out_dram", (B, T, C), F32, kind="ExternalOutput").ap()
    build_kernel(nc, out=out, **aps)
    r = run_bass_kernel_spmd(nc, [arrays], core_ids=[0])
    return r.results[0]["out_dram"]
```
